# Optimizing a Trainium2 kernel written in Bass

```python
import numpy as np
import jax
import jax.numpy as jnp

def _softmax(x, axis=-1):
    return jax.nn.softmax(x, axis=axis)

def _gelu(x):
    return jax.nn.gelu(x, approximate=True)

def _silu(x):
    return jax.nn.silu(x)

def _sigmoid(x):
    return jax.nn.sigmoid(x)

def _layernorm(x, axis=-1, eps=1e-05):
    m = jnp.mean(x, axis=axis, keepdims=True)
    v = jnp.var(x, axis=axis, keepdims=True)
    return (x - m) / jnp.sqrt(v + eps)

def _scatter_add(tgt, idx, src, axis=0):
    return tgt.at[idx].add(src)

def _segment_sum(src, seg, n):
    return jax.ops.segment_sum(src, seg, n)
kernel_name = 'mk_prb_d2_jaxref_r8_463eee'

def setup_inputs(seed: int=0):
    np.random.seed(seed)
    _w = jnp.asarray

    def _L0_attn_setup():
        import jax, jax.numpy as jnp
        import numpy as np
        B, S, D, H = (2, 256, 128, 16)
        HD = D // H
        key = jax.random.key(seed)
        ks = jax.random.split(key, 5)
        return {'x': jax.random.normal(ks[0], (B, S, D), dtype=jnp.float32), 'qkv_w': jax.random.normal(ks[1], (3 * D, D), dtype=jnp.float32) * (1.0 / np.sqrt(D)), 'qkv_b': jax.random.normal(ks[2], (3 * D,), dtype=jnp.float32) * 0.02, 'proj_w': jax.random.normal(ks[3], (D, D), dtype=jnp.float32) * (1.0 / np.sqrt(D)), 'proj_b': jax.random.normal(ks[4], (D,), dtype=jnp.float32) * 0.02}
    _L0_attn_in = _L0_attn_setup()

    def _L0_ffn_setup():
        import jax, jax.numpy as jnp
        import numpy as np
        DIM = 128
        HIDDEN = 384
        SCALE = 1.0 / 127.0

        def _dequant(w_int, dtype):
            return w_int.astype(dtype) * jnp.asarray(SCALE, dtype)
        key = jax.random.key(seed)
        k_x, k_g, k_u, k_d = jax.random.split(key, 4)
        x = jax.random.normal(k_x, (4, 256, DIM), dtype=jnp.float32)
        w_gate = jax.random.randint(k_g, (HIDDEN, DIM), -127, 128, dtype=jnp.int32)
        w_up = jax.random.randint(k_u, (HIDDEN, DIM), -127, 128, dtype=jnp.int32)
        w_down = jax.random.randint(k_d, (DIM, HIDDEN), -127, 128, dtype=jnp.int32)
        return {'x': x, 'w_gate': w_gate, 'w_up': w_up, 'w_down': w_down}
    _L0_ffn_in = _L0_ffn_setup()

    def _L1_attn_setup():
        import jax, jax.numpy as jnp
        import numpy as np
        import math
        DIM = 128
        NUM_HEADS = 16
        HEAD_DIM = DIM // NUM_HEADS
        BLOCK_SIZE = 64

        def _block_mask(src_blocks, tgt_blocks, num_blocks):
            i = jnp.arange(num_blocks)[:, None]
            j = jnp.arange(num_blocks)[None, :]
            band = jnp.abs(i - j) <= 1
            glob = (j == 0) | (j == num_blocks - 1)
            bm = band | glob
            bm = bm.at[src_blocks, tgt_blocks].set(True)
            return bm
        key = jax.random.key(seed)
        ks = jax.random.split(key, 12)
        B, S = (2, 256)
        x = jax.random.normal(ks[0], (B, S, DIM), dtype=jnp.float32)
        scale = 0.02
        Wq = jax.random.normal(ks[1], (DIM, DIM), dtype=jnp.float32) * scale
        bq = jnp.zeros((DIM,), dtype=jnp.float32)
        Wk = jax.random.normal(ks[2], (DIM, DIM), dtype=jnp.float32) * scale
        bk = jnp.zeros((DIM,), dtype=jnp.float32)
        Wv = jax.random.normal(ks[3], (DIM, DIM), dtype=jnp.float32) * scale
        bv = jnp.zeros((DIM,), dtype=jnp.float32)
        Wo = jax.random.normal(ks[4], (DIM, DIM), dtype=jnp.float32) * scale
        bo = jnp.zeros((DIM,), dtype=jnp.float32)
        num_blocks = S // BLOCK_SIZE
        src_blocks = jax.random.randint(ks[5], (3,), 0, num_blocks, dtype=jnp.int32)
        tgt_blocks = jax.random.randint(ks[6], (3,), 0, num_blocks, dtype=jnp.int32)
        return {'x': x, 'Wq': Wq, 'bq': bq, 'Wk': Wk, 'bk': bk, 'Wv': Wv, 'bv': bv, 'Wo': Wo, 'bo': bo, 'src_blocks': src_blocks, 'tgt_blocks': tgt_blocks}
    _L1_attn_in = _L1_attn_setup()

    def _L1_ffn_setup():
        import jax, jax.numpy as jnp
        import numpy as np
        NUM_EXPERTS = 8
        TOP_K = 2
        CAPACITY_FACTOR = 1.25
        key = jax.random.key(seed)
        ks = jax.random.split(key, 5)
        B, S, D, H, E = (4, 256, 128, 256, NUM_EXPERTS)
        scale = 0.02
        return {'x': jax.random.normal(ks[0], (B, S, D), dtype=jnp.float32), 'gate_w': jax.random.normal(ks[1], (E, D), dtype=jnp.float32) * scale, 'gate_proj_w': jax.random.normal(ks[2], (E, H, D), dtype=jnp.float32) * scale, 'up_proj_w': jax.random.normal(ks[3], (E, H, D), dtype=jnp.float32) * scale, 'down_proj_w': jax.random.normal(ks[4], (E, D, H), dtype=jnp.float32) * scale}
    _L1_ffn_in = _L1_ffn_setup()
    _d = {'L0_attn_x': _L0_attn_in['x'], 'L0_attn_qkv_w': _L0_attn_in['qkv_w'], 'L0_attn_qkv_b': _L0_attn_in['qkv_b'], 'L0_attn_proj_w': _L0_attn_in['proj_w'], 'L0_attn_proj_b': _L0_attn_in['proj_b'], 'L0_ffn_w_gate': _L0_ffn_in['w_gate'], 'L0_ffn_w_up': _L0_ffn_in['w_up'], 'L0_ffn_w_down': _L0_ffn_in['w_down'], 'L1_attn_Wq': _L1_attn_in['Wq'], 'L1_attn_bq': _L1_attn_in['bq'], 'L1_attn_Wk': _L1_attn_in['Wk'], 'L1_attn_bk': _L1_attn_in['bk'], 'L1_attn_Wv': _L1_attn_in['Wv'], 'L1_attn_bv': _L1_attn_in['bv'], 'L1_attn_Wo': _L1_attn_in['Wo'], 'L1_attn_bo': _L1_attn_in['bo'], 'L1_attn_src_blocks': _L1_attn_in['src_blocks'], 'L1_attn_tgt_blocks': _L1_attn_in['tgt_blocks'], 'L1_ffn_gate_w': _L1_ffn_in['gate_w'], 'L1_ffn_gate_proj_w': _L1_ffn_in['gate_proj_w'], 'L1_ffn_up_proj_w': _L1_ffn_in['up_proj_w'], 'L1_ffn_down_proj_w': _L1_ffn_in['down_proj_w']}
    _x0 = _d['L0_attn_x']
    _d['L0_attn_x'] = jax.random.normal(jax.random.fold_in(jax.random.key(seed), 1), (4, 512, 128), dtype=_x0.dtype)
    del _x0
    return _d

def reference(L0_attn_x, L0_attn_qkv_w, L0_attn_qkv_b, L0_attn_proj_w, L0_attn_proj_b, L0_ffn_w_gate, L0_ffn_w_up, L0_ffn_w_down, L1_attn_Wq, L1_attn_bq, L1_attn_Wk, L1_attn_bk, L1_attn_Wv, L1_attn_bv, L1_attn_Wo, L1_attn_bo, L1_attn_src_blocks, L1_attn_tgt_blocks, L1_ffn_gate_w, L1_ffn_gate_proj_w, L1_ffn_up_proj_w, L1_ffn_down_proj_w):

    def _L0_attn_ref(x, qkv_w, qkv_b, proj_w, proj_b):
        import jax, jax.numpy as jnp
        import numpy as np
        B, S, D, H = (2, 256, 128, 16)
        HD = D // H
        b, s, d = x.shape
        qkv = jnp.einsum('bsd,ed->bse', x, qkv_w) + qkv_b
        qkv = qkv.reshape(b, s, 3, H, HD)
        q = jnp.transpose(qkv[:, :, 0], (0, 2, 1, 3))
        k = jnp.transpose(qkv[:, :, 1], (0, 2, 1, 3))
        v = jnp.transpose(qkv[:, :, 2], (0, 2, 1, 3))
        scale = 1.0 / jnp.sqrt(jnp.asarray(HD, dtype=x.dtype))
        scores = jnp.einsum('bhqe,bhke->bhqk', q, k) * scale
        attn = jax.nn.softmax(scores, axis=-1)
        out = jnp.einsum('bhqk,bhke->bhqe', attn, v)
        out = jnp.transpose(out, (0, 2, 1, 3)).reshape(b, s, d)
        out = jnp.einsum('bsd,ed->bse', out, proj_w) + proj_b
        return out

    def _L0_ffn_ref(x, w_gate, w_up, w_down):
        import jax, jax.numpy as jnp
        import numpy as np
        DIM = 128
        HIDDEN = 384
        SCALE = 1.0 / 127.0

        def _dequant(w_int, dtype):
            return w_int.astype(dtype) * jnp.asarray(SCALE, dtype)
        wg = _dequant(w_gate, x.dtype)
        wu = _dequant(w_up, x.dtype)
        wd = _dequant(w_down, x.dtype)
        gate = jnp.einsum('bsd,hd->bsh', x, wg)
        up = jnp.einsum('bsd,hd->bsh', x, wu)
        h = jax.nn.silu(gate) * up
        return jnp.einsum('bsh,dh->bsd', h, wd)

    def _L1_attn_ref(x, Wq, bq, Wk, bk, Wv, bv, Wo, bo, src_blocks, tgt_blocks):
        import jax, jax.numpy as jnp
        import numpy as np
        import math
        DIM = 128
        NUM_HEADS = 16
        HEAD_DIM = DIM // NUM_HEADS
        BLOCK_SIZE = 64

        def _block_mask(src_blocks, tgt_blocks, num_blocks):
            i = jnp.arange(num_blocks)[:, None]
            j = jnp.arange(num_blocks)[None, :]
            band = jnp.abs(i - j) <= 1
            glob = (j == 0) | (j == num_blocks - 1)
            bm = band | glob
            bm = bm.at[src_blocks, tgt_blocks].set(True)
            return bm
        B, S, _ = x.shape
        nb = S // BLOCK_SIZE
        q = (x @ Wq.T + bq).reshape(B, NUM_HEADS, S, HEAD_DIM)
        k = (x @ Wk.T + bk).reshape(B, NUM_HEADS, S, HEAD_DIM)
        v = (x @ Wv.T + bv).reshape(B, NUM_HEADS, S, HEAD_DIM)
        bm = _block_mask(src_blocks, tgt_blocks, nb)
        mask = jnp.repeat(jnp.repeat(bm, BLOCK_SIZE, axis=0), BLOCK_SIZE, axis=1)
        scores = jnp.einsum('bhqd,bhkd->bhqk', q, k) / math.sqrt(HEAD_DIM)
        scores = jnp.where(mask[None, None], scores, jnp.float32(-1000000000.0))
        attn = jax.nn.softmax(scores, axis=-1)
        out = jnp.einsum('bhqk,bhkd->bhqd', attn, v)
        out = out.transpose(0, 2, 1, 3).reshape(B, S, DIM)
        return out @ Wo.T + bo

    def _L1_ffn_ref(x, gate_w, gate_proj_w, up_proj_w, down_proj_w):
        import jax, jax.numpy as jnp
        import numpy as np
        NUM_EXPERTS = 8
        TOP_K = 2
        CAPACITY_FACTOR = 1.25
        B, S, D = x.shape
        E, K = (NUM_EXPERTS, TOP_K)
        T = B * S
        xf = x.reshape(T, D)
        logits = xf @ gate_w.T
        probs = jax.nn.softmax(logits, axis=-1)
        top_p, top_i = jax.lax.top_k(probs, K)
        w = top_p / (jnp.sum(top_p, axis=-1, keepdims=True) + 1e-09)
        capacity = int(CAPACITY_FACTOR * T / E)
        oh = jax.nn.one_hot(top_i, E, dtype=jnp.int32)
        rank = jnp.cumsum(oh, axis=0) - 1
        my_rank = jnp.sum(rank * oh, axis=-1)
        keep = (my_rank < capacity).astype(w.dtype)
        comb = jnp.einsum('tk,tke->te', w * keep, oh.astype(w.dtype))
        out = jnp.zeros_like(xf)
        for e in range(E):
            g = jax.nn.silu(xf @ gate_proj_w[e].T)
            u = xf @ up_proj_w[e].T
            y = g * u @ down_proj_w[e].T
            out = out + comb[:, e:e + 1] * y
        return out.reshape(B, S, D)
    x = L0_attn_x
    xn = _layernorm(x, axis=-1)
    x = x + _L0_attn_ref(xn, L0_attn_qkv_w, L0_attn_qkv_b, L0_attn_proj_w, L0_attn_proj_b) + _L0_ffn_ref(xn, L0_ffn_w_gate, L0_ffn_w_up, L0_ffn_w_down)
    xn = _layernorm(x, axis=-1)
    x = x + _L1_attn_ref(xn, L1_attn_Wq, L1_attn_bq, L1_attn_Wk, L1_attn_bk, L1_attn_Wv, L1_attn_bv, L1_attn_Wo, L1_attn_bo, L1_attn_src_blocks, L1_attn_tgt_blocks) + _L1_ffn_ref(xn, L1_ffn_gate_w, L1_ffn_gate_proj_w, L1_ffn_up_proj_w, L1_ffn_down_proj_w)
    return x

_drawn_inputs = setup_inputs


def setup_inputs(seed=0):
    import zlib

    import numpy as np

    out = dict(_drawn_inputs(seed))
    spreads = {'L1_attn_bq': (0.0, 2.0),
     'L1_attn_bk': (0.0, 2.0),
     'L1_attn_bv': (0.0, 2.0),
     'L1_attn_bo': (0.0, 2.0)}
    factors = {'L0_attn_qkv_w': 8.0,
     'L0_attn_qkv_b': 8.0,
     'L0_attn_proj_w': 8.0,
     'L0_attn_proj_b': 64.0,
     'L1_attn_Wq': 64.0,
     'L1_attn_Wk': 64.0,
     'L1_attn_Wv': 64.0,
     'L1_attn_Wo': 64.0,
     'L1_ffn_gate_w': 40.111,
     'L1_ffn_gate_proj_w': 40.399,
     'L1_ffn_up_proj_w': 36.351,
     'L1_ffn_down_proj_w': 36.332}
    for name, (base, spread) in spreads.items():
        noise = np.random.default_rng([zlib.crc32(name.encode()), seed]).standard_normal(out[name].shape)
        drawn = base * np.exp(spread * noise) if base else spread * noise
        out[name] = jnp.asarray(drawn.astype(out[name].dtype))
    for name, factor in factors.items():
        out[name] = (out[name] * factor).astype(out[name].dtype)
    return out
```

```python
from contextlib import ExitStack

import concourse.bass as bass
from concourse import mybir

F32 = mybir.dt.float32
BF16 = mybir.dt.bfloat16
I32 = mybir.dt.int32
ALU = mybir.AluOpType
ACT = mybir.ActivationFunctionType
AX_X = mybir.AxisListType.X

P = 128
EPS = 1e-5
MASKED = -1e30


def build(nc, x, qkv_wT, qkv_b, proj_wT, proj_b, wg_T, wu_T, wd_T, Wq_T, bq, Wk_T, bk, Wv_T, bv, Wo_T, bo,
          src_blocks, tgt_blocks, router_T, eg_T, eu_T, ed_T, out):
    B, S, D = x.shape
    H, HD = 16, 8
    NT = S // P
    G = 4
    STEPS = H // G
    HID = wg_T.shape[1]
    HB = HID // P
    E, EH = eg_T.shape[1], eg_T.shape[2]
    EB = EH // P
    T = B * S
    CAP = int(1.25 * T / E)
    NB = S // 64
    SLOT = 64
    ROWS = 96
    M_ROW, MASK_ROW = 48, 64
    QSCALE = HD ** -0.5
    NSRC = src_blocks.shape[0]

    x_mid = nc.dram_tensor("x_mid", (B, S, D), F32, kind="Internal").ap()
    v_bounce = nc.dram_tensor("v_bounce", (S, D), F32, kind="Internal").ap()

    with ExitStack() as ctx:
        def sb(name, shape, dt=F32):
            return ctx.enter_context(nc.sbuf_tensor(name, shape, dt))

        def sem(name):
            return ctx.enter_context(nc.semaphore(name))

        ident = sb("ident", [P, P])
        ident_bf = sb("ident_bf", [P, P], BF16)
        zero_bf = sb("zero_bf", [P, NT * H, HD], BF16)
        tri = sb("tri", [P, P], BF16)
        ones_bf = sb("ones_bf", [P, P], BF16)
        w_qkv = [sb("w_qkv0", [P, 3 * D]), sb("w_qkv1", [P, 3 * D])]
        b_qkv = [sb("b_qkv0", [P, 3 * D]), sb("b_qkv1", [P, 3 * D])]
        w_proj = [sb("w_proj0", [P, D]), sb("w_proj1", [P, D])]
        b_proj = [sb("b_proj0", [P, D]), sb("b_proj1", [P, D])]
        wg_i = sb("wg_i", [P, HID], I32)
        wu_i = sb("wu_i", [P, HID], I32)
        wd_i = sb("wd_i", [P, HB, D], I32)
        wg = sb("wg", [P, HID])
        wu = sb("wu", [P, HID])
        wd = sb("wd", [P, HB, D])
        w_router = sb("w_router", [P, E])
        eg = sb("eg", [P, E, EH])
        eu = sb("eu", [P, E, EH])
        ed = sb("ed", [P, E, EB, D])
        st_i = sb("st_i", [NB, 2, NSRC], I32)
        st_f = sb("st_f", [NB, 2, NSRC])
        blk_q = sb("blk_q", [NB, NB])
        blk_k = sb("blk_k", [NB, NB])
        hits = sb("hits", [NB, NB])
        tmp8 = sb("tmp8", [NB, 4, NB])
        mask_q = sb("mask_q", [NB, S], BF16)
        onehot_k = sb("onehot_k", [NB, S], BF16)
        x_in = sb("x_in", [P, NT, D])
        x_out = sb("x_out", [P, NT, D])
        stats = sb("stats", [P, NT, 6])
        mv = sb("mv", [P, NT, 2])
        rstd = sb("rstd", [P, NT])
        var_eps = sb("var_eps", [P, NT])
        eps_t = sb("eps_t", [P, NT])
        neg_half = sb("neg_half", [P, NT])
        wait_taker = sb("wait_taker", [P, NT])
        xn = sb("xn", [P, NT, D])
        xnT = sb("xnT", [P, S])
        qk = sb("qk", [P, 2, NT, D])
        part = [sb(f"part{i}", [P, 2, NT * H, HD], BF16) for i in range(3)]
        rest = [sb(f"rest{i}", [P, 2, NT, D]) for i in range(2)]
        v_nat = sb("v_nat", [P, NT, D])
        Rq = sb("Rq", [P, NT * H, SLOT], BF16)
        Rk = sb("Rk", [P, NT * H, SLOT], BF16)
        QO = sb("QO", [ROWS, H, S], BF16)
        KO = sb("KO", [ROWS, H, S], BF16)
        Vp = sb("Vp", [P, NT, H, 32])
        PT = sb("PT", [P, 4, 2, S])
        mx = sb("mx", [P, 2, NT, G])
        mr = sb("mr", [P, 2, NT, G])
        mp = sb("mp", [P, 2, NT, 3, G], BF16)
        mT = sb("mT", [3 * G, 2, S], BF16)
        o_sb = sb("o_sb", [P, 2, S])
        rden = sb("rden", [P, NT * 2, G, 2])
        o_nat = sb("o_nat", [P, NT, D])
        o_T = sb("o_T", [P, S])
        sil = sb("sil", [P, 2, S])
        hT = sb("hT", [P, 2, max(HB, EB), S])
        iota_e = sb("iota_e", [P, NT, E])
        iota_hi = sb("iota_hi", [P, NT, E])
        r_p = sb("r_p", [P, NT, E])
        r_t = sb("r_t", [P, 4, NT, E])
        r_s = sb("r_s", [P, 8, NT])
        oh = sb("oh", [P, NT, 2, E], BF16)
        rk = sb("rk", [P, NT, 2 * E])
        tot = sb("tot", [P, NT, 2 * E])
        carry = sb("carry", [P, 2, 2 * E])
        comb = sb("comb", [P, NT, E])

        ps = ctx.enter_context(nc.psum_tensor("ps", [P, 8, 512], F32))

        def ps_bf(bank):
            return ps[:, bank, :].bitcast(BF16)

        MX_BANK, PV_BANK, MT_BANK = 4, 6, 7

        loaded = sem("loaded")
        consts = sem("consts")
        cleared = sem("cleared")
        dve_setup = sem("dve_setup")
        ready = sem("ready")
        rows_in = sem("rows_in")
        mask_ready = sem("mask_ready")

        block = ctx.enter_context(nc.Block())

        loads = [(w_qkv[0][:], qkv_wT), (b_qkv[0][:], qkv_b[None, :].to_broadcast([P, 3 * D])),
                 (w_proj[0][:], proj_wT), (b_proj[0][:], proj_b[None, :].to_broadcast([P, D])),
                 (wg_i[:], wg_T), (wu_i[:], wu_T), (wd_i[:], wd_T.rearrange("(b p) d -> p b d", p=P)),
                 (w_proj[1][:], Wo_T), (b_proj[1][:], bo[None, :].to_broadcast([P, D])),
                 (w_router[:], router_T), (eg[:], eg_T), (eu[:], eu_T),
                 (ed[:], ed_T.rearrange("e (b p) d -> p e b d", p=P)),
                 (st_i[:, 0, :], src_blocks[None, :].to_broadcast([NB, NSRC])),
                 (st_i[:, 1, :], tgt_blocks[None, :].to_broadcast([NB, NSRC]))]
        for i, (w, b) in enumerate(((Wq_T, bq), (Wk_T, bk), (Wv_T, bv))):
            loads.append((w_qkv[1][:, i * D:(i + 1) * D], w))
            loads.append((b_qkv[1][:, i * D:(i + 1) * D], b[None, :].to_broadcast([P, D])))
        N_LOAD = 16 * len(loads)

        def setup_sync(sp):
            for dst, src in loads:
                sp.dma_start(dst, src).then_inc(loaded, 16)

        def setup_pool(pool):
            for n, t in enumerate((ident, ident_bf)):
                pool.memset(t[:], 0.0).then_inc(consts, 1)
                pool.wait_ge(consts, 2 * n + 1)
                pool.affine_select(out=t[:], in_=t[:], compare_op=ALU.not_equal, fill=1.0, base=0,
                                   pattern=[[-1, P]], channel_multiplier=1).then_inc(consts, 1)
            pool.memset(tri[:], 1.0).then_inc(consts, 1)
            pool.wait_ge(consts, 5)
            pool.affine_select(out=tri[:], in_=tri[:], compare_op=ALU.is_ge, fill=0.0, base=0,
                               pattern=[[1, P]], channel_multiplier=-1).then_inc(consts, 1)
            pool.memset(ones_bf[:], 1.0).then_inc(consts, 1)
            pool.iota(iota_e[:], pattern=[[0, NT], [1, E]], base=0, channel_multiplier=0,
                      allow_small_or_imprecise_dtypes=True).then_inc(consts, 1)
            pool.iota(iota_hi[:], pattern=[[0, NT], [1, E]], base=99, channel_multiplier=0,
                      allow_small_or_imprecise_dtypes=True).then_inc(consts, 1)
            pool.iota(blk_q[:], pattern=[[1, NB]], base=0, channel_multiplier=0,
                      allow_small_or_imprecise_dtypes=True).then_inc(consts, 1)
            pool.iota(blk_k[:], pattern=[[0, NB]], base=0, channel_multiplier=1,
                      allow_small_or_imprecise_dtypes=True).then_inc(consts, 1)
            pool.memset(onehot_k[:], 1.0).then_inc(consts, 1)
            pool.wait_ge(consts, 12)
            pool.affine_select(out=onehot_k[:], in_=onehot_k[:], compare_op=ALU.is_ge, fill=0.0, base=0,
                               pattern=[[1, S]], channel_multiplier=-64).then_inc(consts, 1)
            pool.wait_ge(consts, 13)
            pool.affine_select(out=onehot_k[:], in_=onehot_k[:], compare_op=ALU.is_ge, fill=0.0, base=63,
                               pattern=[[-1, S]], channel_multiplier=64).then_inc(consts, 1)
            pool.memset(zero_bf[:], 0.0)
            pool.memset(eps_t[:], EPS)
            pool.memset(neg_half[:], -0.5)
            pool.memset(Rk[:], 0.0).then_inc(cleared, 1)
            pool.memset(Rq[:], 0.0).then_inc(cleared, 1)
            pool.wait_ge(cleared, 2)
            pool.memset(Rk[:, :, M_ROW:M_ROW + 3], 1.0).then_inc(cleared, 1)
            pool.memset(Vp[:], 0.0).then_inc(cleared, 1)
            pool.wait_ge(cleared, 4)
            for c in range(2):
                pool.memset(Vp[:, :, c:H:2, 16 + c:17 + c], 1.0).then_inc(cleared, 1)
            pool.wait_ge(cleared, N_CLEARED)

        N_CONST, N_CLEARED = 14, 6

        def setup_vector(dve):
            n = [0]

            def link(ins):
                n[0] += 1
                ins.then_inc(dve_setup, 1)
                dve.wait_ge(dve_setup, n[0])

            dve.memset(QO[64:96], 0.0)
            dve.memset(KO[64:96], 0.0)
            dve.memset(carry[:], 0.0).then_inc(dve_setup, 1)
            n[0] += 1
            dve.wait_ge(loaded, N_LOAD)
            for i, f, w in ((wg_i, wg, None), (wu_i, wu, None), (wd_i, wd, None)):
                link(dve.tensor_copy(f[:], i[:]))
                dve.tensor_scalar(f[:], f[:], 1.0 / 127.0, None, ALU.mult)
            for layer in range(2):
                dve.tensor_scalar(w_qkv[layer][:, 0:D], w_qkv[layer][:, 0:D], QSCALE, None, ALU.mult)
                dve.tensor_scalar(b_qkv[layer][:, 0:D], b_qkv[layer][:, 0:D], QSCALE, None, ALU.mult)
            link(dve.tensor_copy(st_f[:], st_i[:]))
            dve.wait_ge(consts, N_CONST)
            link(dve.tensor_tensor(tmp8[:, 0, :], blk_q[:], blk_k[:], ALU.subtract))
            link(dve.tensor_tensor(tmp8[:, 1, :], tmp8[:, 0, :], tmp8[:, 0, :], ALU.mult))
            link(dve.tensor_scalar(hits[:], tmp8[:, 1, :], 1.0, None, ALU.is_le))
            for j in (0, NB - 1):
                link(dve.tensor_scalar(tmp8[:, 0, :], blk_k[:], float(j), None, ALU.is_equal))
                link(dve.tensor_tensor(hits[:], hits[:], tmp8[:, 0, :], ALU.add))
            for n_pair in range(NSRC):
                for side, blk in ((0, blk_q), (1, blk_k)):
                    v = st_f[:, side, n_pair:n_pair + 1]
                    link(dve.tensor_scalar(tmp8[:, 2, :], blk[:], v, None, ALU.is_equal))
                    link(dve.tensor_scalar(tmp8[:, 3, :], blk[:], float(NB), v, ALU.subtract, ALU.is_equal))
                    link(dve.tensor_tensor(tmp8[:, side, :], tmp8[:, 2, :], tmp8[:, 3, :], ALU.add))
                link(dve.tensor_tensor(tmp8[:, 0, :], tmp8[:, 0, :], tmp8[:, 1, :], ALU.mult))
                link(dve.tensor_tensor(hits[:], hits[:], tmp8[:, 0, :], ALU.add))
            link(dve.tensor_scalar(hits[:], hits[:], 0.5, MASKED, ALU.is_lt, ALU.mult))
            dve.tensor_copy(mask_q[:].rearrange("p (b t) -> p b t", b=NB),
                            hits[:].unsqueeze(2).to_broadcast([NB, NB, 64])).then_inc(mask_ready, 1)
            dve.wait_ge(cleared, N_CLEARED)
            dve.tensor_copy(tmp8[:, 0, :], blk_q[:]).then_inc(ready, 1)

        def layer(L):
            x_src = x if L == 0 else x_mid
            x_dst = x_mid if L == 0 else out
            units = f"L{L}"

            x_loaded = sem("x_loaded" + units)
            dve_c = sem("dve_c" + units)
            act_c = sem("act_c" + units)
            mv_ready = sem("mv_ready" + units)
            rstd_ready = sem("rstd_ready" + units)
            xn_ready = sem("xn_ready" + units)
            xnT_ps = sem("xnT_ps" + units)
            xnT_ready = sem("xnT_ready" + units)
            qkv_ps = sem("qkv_ps" + units)
            qk_ready = sem("qk_ready" + units)
            v_ready = sem("v_ready" + units)
            v_stored = sem("v_stored" + units)
            v_loaded = sem("v_loaded" + units)
            p1_ready = sem("p1_ready" + units)
            p2_ready = sem("p2_ready" + units)
            p3_ready = sem("p3_ready" + units)
            r1_ready = sem("r1_ready" + units)
            r2_ready = sem("r2_ready" + units)
            R_ready = sem("R_ready" + units)
            RT_ps = sem("RT_ps" + units)
            q_copied = sem("q_copied" + units)
            k_copied = sem("k_copied" + units)
            max_ps = sem("max_ps" + units)
            max_read = sem("max_read" + units)
            m_split = sem("m_split" + units)
            mT_ps = sem("mT_ps" + units)
            mT_ready = sem("mT_ready" + units)
            m_rows = sem("m_rows" + units)
            st_ps = sem("st_ps" + units)
            exp_done = sem("exp_done" + units)
            pv_done = sem("pv_done" + units)
            o_copied = sem("o_copied" + units)
            oT_ps = sem("oT_ps" + units)
            on_ready = sem("on_ready" + units)
            onT_ps = sem("onT_ps" + units)
            onT_ready = sem("onT_ready" + units)
            gate_ps = sem("gate_ps" + units)
            up_ps = sem("up_ps" + units)
            silu_done = sem("silu_done" + units)
            h_ready = sem("h_ready" + units)
            y_ps = sem("y_ps" + units)
            y_read = sem("y_read" + units)
            base_read = sem("base_read" + units)
            out_ready = sem("out_ready" + units)
            stored = sem("stored" + units)
            logit_ps = sem("logit_ps" + units)
            lg_ready = sem("lg_ready" + units)
            rexp_done = sem("rexp_done" + units)
            oh_ready = sem("oh_ready" + units)
            rank_ps = sem("rank_ps" + units)

            NG = HB if L == 0 else E * EB
            EXPS = 2 * NT

            def head(s, g):
                return 4 * g + s

            def weights(n):
                if L == 0:
                    return wg[:, n * P:(n + 1) * P], wu[:, n * P:(n + 1) * P]
                e, i = n // EB, n % EB
                return eg[:, e, i * P:(i + 1) * P], eu[:, e, i * P:(i + 1) * P]

            GU = ((0, 1), (2, 3))

            def sync_program(sp):
                if L == 1:
                    sp.wait_ge(mask_ready, 1)
                    sp.wait_ge(ready, 1)
                    for h in range(H):
                        sp.dma_start(QO[MASK_ROW:MASK_ROW + NB, h, :], mask_q[:]).then_inc(rows_in, 16)
                        sp.dma_start(KO[MASK_ROW:MASK_ROW + NB, h, :], onehot_k[:]).then_inc(rows_in, 16)
                sp.sem_inc(stored, 16)
                with sp.Fori(0, B) as b:
                    sp.wait_ge(stored, 16 * b + 16)
                    sp.dma_start(x_in[:], x_src[b].rearrange("(t p) d -> p t d", p=P)).then_inc(x_loaded, 16)
                    if L == 1:
                        sp.wait_ge(v_ready, b + 1)
                        sp.dma_start(v_bounce.rearrange("(t p) d -> p t d", p=P), v_nat[:]).then_inc(v_stored, 16)
                        sp.wait_ge(v_stored, 16 * b + 16)
                        v_pos = v_bounce.rearrange("(h k t) (c d) -> k (t c) h d", h=H, k=NT, c=H)
                        for k in range(NT):
                            for c in range(2):
                                sp.dma_start(Vp[:, k, c:H:2, HD * c:HD * c + HD],
                                             v_pos[k][:, c:H:2, :]).then_inc(v_loaded, 16)
                    for s in range(STEPS):
                        sp.wait_ge(mT_ready, STEPS * b + s + 1)
                        for i in range(3):
                            for g in range(G):
                                sp.dma_start(QO[M_ROW + i:M_ROW + i + 1, head(s, g), :],
                                             mT[G * i + g:G * i + g + 1, s % 2, :]).then_inc(m_rows, 16)
                    if L == 0:
                        sp.wait_ge(out_ready, b + 1)
                    else:
                        sp.wait_ge(y_read, E * b + E)
                    sp.dma_start(x_dst[b].rearrange("(t p) d -> p t d", p=P), x_out[:]).then_inc(stored, 16)

            def pool_program(pool):
                with pool.Fori(0, B) as b:
                    p1, p2, p3 = part
                    pool.wait_ge(mv_ready, b + 1)
                    pool.tensor_tensor(var_eps[:], mv[:, :, 1], eps_t[:], ALU.add).then_inc(rstd_ready, 1)
                    pool.wait_ge(rstd_ready, 2 * b + 1)
                    pool.tensor_tensor(rstd[:], var_eps[:], neg_half[:], ALU.pow).then_inc(rstd_ready, 1)
                    pool.wait_ge(p1_ready, b + 1)
                    Rq_s = Rq[:, :, 0:48].rearrange("p n (s d) -> p n s d", d=HD)
                    Rk_s = Rk[:, :, 0:48].rearrange("p n (s d) -> p n s d", d=HD)
                    for i in (0, 1, 2):
                        pool.tensor_tensor(Rq_s[:, :, i, :], p1[:, 0], zero_bf[:], ALU.add).then_inc(R_ready, 1)
                    for i in (0, 3, 5):
                        pool.tensor_tensor(Rk_s[:, :, i, :], p1[:, 1], zero_bf[:], ALU.add).then_inc(R_ready, 1)
                    pool.wait_ge(p2_ready, b + 1)
                    for i in (3, 4):
                        pool.tensor_tensor(Rq_s[:, :, i, :], p2[:, 0], zero_bf[:], ALU.add).then_inc(R_ready, 1)
                    for i in (1, 4):
                        pool.tensor_tensor(Rk_s[:, :, i, :], p2[:, 1], zero_bf[:], ALU.add).then_inc(R_ready, 1)
                    pool.wait_ge(p3_ready, b + 1)
                    pool.tensor_tensor(Rq_s[:, :, 5, :], p3[:, 0], zero_bf[:], ALU.add).then_inc(R_ready, 1)
                    pool.tensor_tensor(Rk_s[:, :, 2, :], p3[:, 1], zero_bf[:], ALU.add).then_inc(R_ready, 1)

            def last_stores(sp):
                sp.wait_ge(stored, 16 * B + 16)

            def operand_copy(eng_copy, bank, buf, j, r):
                src = ps_bf(bank)[SLOT * r:SLOT * r + SLOT, :].rearrange("p (a n) -> p a n", a=2)
                if L == 0:
                    h0 = 4 * j + r
                    return eng_copy(buf[0:SLOT, h0:h0 + 3:2, :], src)
                dst = buf[0:SLOT].rearrange("p h (t c) -> p c (h t)", c=H)
                c0 = 4 * j + r
                return eng_copy(dst[:, c0:c0 + 3:2, :], src)

            def tensor_program(pe):
                if L == 0:
                    pe.wait_ge(consts, N_CONST)
                    pe.wait_ge(ready, 1)
                    pe.wait_ge(cleared, N_CLEARED)
                else:
                    pe.wait_ge(rows_in, 32 * H)
                with pe.Fori(0, B) as b:
                    pe.wait_ge(xn_ready, b + 1)
                    for t in range(NT):
                        last = pe.transpose(ps[:, MT_BANK, t * P:(t + 1) * P], xn[:, t, :], ident[:])
                    last.then_inc(xnT_ps, 1)
                    pe.wait_ge(xnT_ready, b + 1)
                    for t in range(NT):
                        pe.matmul(ps[:, t, 0:3 * D], xnT[:, t * P:(t + 1) * P], w_qkv[L][:],
                                  start=True, stop=True).then_inc(qkv_ps, 1)
                    pe.wait_ge(R_ready, 12 * b + 12)
                    for n, R in enumerate((Rq, Rk)):
                        Rv = R[:].rearrange("p (t h) s -> p t (h s)", t=NT)
                        for j in range(4):
                            for a in range(2):
                                for t in range(NT):
                                    c0 = (2 * j + a) * 2 * SLOT
                                    last = pe.transpose(ps_bf(4 * n + j)[:, a * S + t * P:a * S + (t + 1) * P],
                                                        Rv[:, t, c0:c0 + 2 * SLOT], ident_bf[:])
                            last.then_inc(RT_ps, 1)
                    pe.wait_ge(q_copied, 8 * b + 8)
                    pe.wait_ge(k_copied, 8 * b + 8)

                    def max_mm(s, n):
                        qt, g = n // G, n % G
                        if s > 0 or n >= 2:
                            pe.wait_ge(max_read, 64 * b + 16 * s + n - 1)
                        h = head(s, g)
                        pe.matmul(ps[:, MX_BANK + n % 2, :], QO[:, h, qt * P:(qt + 1) * P], KO[:, h, :],
                                  start=True, stop=True).then_inc(max_ps, 1)

                    def m_transposes(s):
                        pe.wait_ge(m_split, STEPS * b + s + 1)
                        for t in range(NT):
                            last = pe.transpose(ps_bf(MT_BANK)[0:3 * G, t * P:(t + 1) * P],
                                                mp[:, s % 2, t].rearrange("p i g -> p (i g)"), ident_bf[:])
                        last.then_inc(mT_ps, 1)

                    def score_mm(s, k, g):
                        n = 2 * k + g // 2
                        if g % 2 == 0 and (s > 0 or n >= 2):
                            pe.wait_ge(exp_done, EXPS * (STEPS * b + s) + n - 1)
                        h = head(s, g)
                        mm = pe.matmul(ps[:, 2 * (n % 2) + g % 2, :], KO[:, h, k * P:(k + 1) * P], QO[:, h, :],
                                       start=True, stop=True)
                        if g % 2 == 1:
                            mm.then_inc(st_ps, 1)

                    def value_mms(s, k):
                        pe.wait_ge(exp_done, EXPS * (STEPS * b + s) + 2 * k + 2)
                        if s == 2 and k == 0:
                            pe.wait_ge(o_copied, 2 * b + 1)
                        if L == 1 and s == 0 and k == 0:
                            pe.wait_ge(v_loaded, 128 * b + 128)
                        for g in range(G):
                            last = pe.matmul(ps[32 * g:32 * g + 32, PV_BANK, :], Vp[:, k, head(s, g), :],
                                             PT[:, (2 * k + g // 2) % 4, g % 2, :],
                                             start=(s % 2 == 0 and k == 0), stop=(s % 2 == 1 and k == NT - 1))
                        last.then_inc(pv_done, 1)

                    for n in range(16):
                        max_mm(0, n)
                    for s in range(STEPS):
                        m_transposes(s)
                        pe.wait_ge(m_rows, 16 * 12 * (STEPS * b + s + 1))
                        for k in range(NT):
                            for g in range(G):
                                if s + 1 < STEPS:
                                    max_mm(s + 1, 4 * k + g)
                                score_mm(s, k, g)
                            if k > 0:
                                value_mms(s, k - 1)
                        value_mms(s, NT - 1)
                    pe.wait_ge(o_copied, 2 * b + 2)
                    for t in range(NT):
                        for a in range(2):
                            c0 = ((t % 2) * 2 + a) * P
                            last = pe.transpose(ps[:, 4 + t // 2, c0:c0 + P], o_sb[:, a, t * P:(t + 1) * P], ident[:])
                    last.then_inc(oT_ps, 1)
                    if L == 1:
                        for t in range(NT):
                            last = pe.matmul(ps[:, MT_BANK, t * E:(t + 1) * E], xnT[:, t * P:(t + 1) * P], w_router[:],
                                             start=True, stop=True)
                        last.then_inc(logit_ps, 1)

                    def gate_up(n):
                        g_bank, u_bank = GU[n % 2]
                        w_g, w_u = weights(n)
                        if n >= 2:
                            pe.wait_ge(silu_done, NG * b + n - 1)
                        pe.matmul(ps[:, g_bank, :], w_g, xnT[:], start=True, stop=True).then_inc(gate_ps, 1)
                        if n >= 2:
                            pe.wait_ge(h_ready, NG * b + n - 1)
                        pe.matmul(ps[:, u_bank, :], w_u, xnT[:], start=True, stop=True).then_inc(up_ps, 1)

                    if L == 0:
                        for n in range(HB):
                            gate_up(n)
                        pe.wait_ge(on_ready, b + 1)
                        for t in range(NT):
                            last = pe.transpose(ps[:, 6, t * P:(t + 1) * P], o_nat[:, t, :], ident[:])
                        last.then_inc(onT_ps, 1)
                        pe.wait_ge(onT_ready, b + 1)
                        pe.wait_ge(h_ready, NG * b + NG)
                        for t in range(NT):
                            tok = slice(t * P, (t + 1) * P)
                            pe.matmul(ps[:, 7, tok], o_T[:, tok], w_proj[L][:], start=True, stop=False)
                            for i in range(HB):
                                last = pe.matmul(ps[:, 7, tok], hT[:, 0, i, tok], wd[:, i, :],
                                                 start=False, stop=(i == HB - 1))
                        last.then_inc(y_ps, 1)
                    else:
                        for n in range(EB):
                            gate_up(n)
                        pe.wait_ge(oh_ready, b + 1)
                        oh2 = oh[:].rearrange("p t k e -> p (t k e)")
                        NOH = NT * 2 * E
                        pe.matmul(ps[:, MT_BANK, 64:64 + NOH], tri[:], oh2, start=True, stop=True)
                        pe.matmul(ps[:, MT_BANK, 128:128 + NOH], ones_bf[:], oh2,
                                  start=True, stop=True).then_inc(rank_ps, 1)
                        pe.wait_ge(on_ready, b + 1)
                        for t in range(NT):
                            last = pe.transpose(ps[:, 6, t * P:(t + 1) * P], o_nat[:, t, :], ident[:])
                        last.then_inc(onT_ps, 1)
                        pe.wait_ge(onT_ready, b + 1)
                        for t in range(NT):
                            tok = slice(t * P, (t + 1) * P)
                            last = pe.matmul(ps[:, 6, tok], o_T[:, tok], w_proj[L][:], start=True, stop=True)
                        last.then_inc(y_ps, 1)
                        for e in range(E):
                            if e + 1 < E:
                                for i in range(EB):
                                    gate_up((e + 1) * EB + i)
                            pe.wait_ge(h_ready, NG * b + (e + 1) * EB)
                            if e >= 2:
                                pe.wait_ge(y_read, E * b + e - 1)
                            for t in range(NT):
                                tok = slice(t * P, (t + 1) * P)
                                for i in range(EB):
                                    last = pe.matmul(ps[:, 4 + e % 2, tok], hT[:, e % 2, i, tok], ed[:, e, i, :],
                                                     start=(i == 0), stop=(i == EB - 1))
                            last.then_inc(y_ps, 1)

            def scalar_program(act):
                with act.Fori(0, B) as b:
                    act.wait_ge(xnT_ps, b + 1)
                    act.copy(xnT[:], ps[:, MT_BANK, :]).then_inc(xnT_ready, 1)
                    flat = [t[:].rearrange("p q n d -> p (q n d)") for t in part]
                    act.wait_ge(qk_ready, b + 1)
                    act.copy(flat[0], qk[:].rearrange("p q t d -> p (q t d)")).then_inc(p1_ready, 1)
                    act.wait_ge(r1_ready, b + 1)
                    act.copy(flat[1], rest[0][:].rearrange("p q t d -> p (q t d)")).then_inc(p2_ready, 1)
                    act.wait_ge(r2_ready, b + 1)
                    act.copy(flat[2], rest[1][:].rearrange("p q t d -> p (q t d)")).then_inc(p3_ready, 1)
                    for j in range(4):
                        act.wait_ge(RT_ps, 8 * b + j + 1)
                        for r in range(2):
                            operand_copy(act.copy, j, QO, j, r).then_inc(q_copied, 1)
                    for s in range(STEPS):
                        act.wait_ge(mT_ps, STEPS * b + s + 1)
                        act.copy(mT[:, s % 2, :], ps_bf(MT_BANK)[0:3 * G, 0:S]).then_inc(mT_ready, 1)
                        for n in range(EXPS):
                            act.wait_ge(st_ps, EXPS * (STEPS * b + s) + n + 1)
                            if s > 0 or n >= 4:
                                act.wait_ge(pv_done, NT * (STEPS * b + s) + n // 2 - 1)
                            act.activation(PT[:, n % 4], ps[:, 2 * (n % 2):2 * (n % 2) + 2, :],
                                           ACT.Exp).then_inc(exp_done, 1)
                        if s % 2 == 1:
                            act.wait_ge(pv_done, NT * (STEPS * b + s + 1))
                            act.copy(o_sb[:, s // 2, :], ps[:, PV_BANK, :]).then_inc(o_copied, 1)

                    def silu(n):
                        act.wait_ge(gate_ps, NG * b + n + 1)
                        if n >= 2:
                            act.wait_ge(h_ready, NG * b + n - 1)
                        act.activation(sil[:, n % 2, :], ps[:, GU[n % 2][0], :], ACT.Silu).then_inc(silu_done, 1)

                    def onT_copy():
                        act.wait_ge(onT_ps, b + 1)
                        act.copy(o_T[:], ps[:, 6, :]).then_inc(onT_ready, 1)

                    if L == 0:
                        for n in range(NG):
                            silu(n)
                        onT_copy()
                    else:
                        act.wait_ge(lg_ready, b + 1)
                        act.activation(r_t[:, 1], r_t[:, 0], ACT.Exp).then_inc(rexp_done, 1)
                        for n in range(EB):
                            silu(n)
                        onT_copy()
                        for n in range(EB, NG):
                            silu(n)

            def vector_program(dve):
                CH = 55 if L == 1 else 19
                with dve.Fori(0, B) as b:
                    n_link = [0]

                    def link(ins):
                        n_link[0] += 1
                        ins.then_inc(dve_c, 1)
                        dve.wait_ge(dve_c, CH * b + n_link[0])

                    dve.wait_ge(x_loaded, 16 * b + 16)
                    for t in range(NT):
                        last = dve.bn_stats(stats[:, t, :], x_in[:, t, :])
                    link(last)
                    dve.tensor_copy(wait_taker[:], eps_t[:])
                    for t in range(NT):
                        last = dve.bn_aggr(mv[:, t, :], stats[:, t, :])
                    last.then_inc(mv_ready, 1)
                    dve.wait_ge(rstd_ready, 2 * b + 2)
                    for t in range(NT):
                        last = dve.tensor_scalar(xn[:, t, :], x_in[:, t, :], mv[:, t, 0:1], rstd[:, t:t + 1],
                                                 ALU.subtract, ALU.mult)
                    last.then_inc(xn_ready, 1)
                    dve.wait_ge(qkv_ps, NT * b + NT)
                    for i in range(2):
                        last = dve.tensor_tensor(qk[:, i], ps[:, 0:NT, i * D:(i + 1) * D],
                                                 b_qkv[L][:, i * D:(i + 1) * D].unsqueeze(1).to_broadcast([P, NT, D]),
                                                 ALU.add)
                    last.then_inc(qk_ready, 1)
                    if L == 0:
                        for c in range(2):
                            for t in range(NT):
                                src = ps[:, t, 2 * D:3 * D].rearrange("p (h c d) -> p c h d", c=2, d=HD)[:, c]
                                bias = b_qkv[L][:, 2 * D:3 * D].rearrange("p (h c d) -> p c h d", c=2, d=HD)[:, c]
                                dve.tensor_tensor(Vp[:, t, c:H:2, HD * c:HD * c + HD], src, bias, ALU.add)
                    else:
                        dve.tensor_tensor(v_nat[:], ps[:, 0:NT, 2 * D:3 * D],
                                          b_qkv[L][:, 2 * D:3 * D].unsqueeze(1).to_broadcast([P, NT, D]),
                                          ALU.add).then_inc(v_ready, 1)
                    pf = [t[:].rearrange("p q n d -> p (q n d)") for t in part]
                    rf = [t[:].rearrange("p q t d -> p (q t d)") for t in rest]
                    dve.wait_ge(p1_ready, b + 1)
                    dve.tensor_tensor(rf[0], qk[:].rearrange("p q t d -> p (q t d)"), pf[0],
                                      ALU.subtract).then_inc(r1_ready, 1)
                    dve.wait_ge(p2_ready, b + 1)
                    dve.wait_ge(r1_ready, b + 1)
                    dve.tensor_tensor(rf[1], rf[0], pf[1], ALU.subtract).then_inc(r2_ready, 1)
                    for j in range(4):
                        dve.wait_ge(RT_ps, 8 * b + 4 + j + 1)
                        for r in range(2):
                            operand_copy(dve.tensor_copy, 4 + j, KO, j, r).then_inc(k_copied, 1)

                    for s in range(STEPS):
                        for n in range(16):
                            dve.wait_ge(max_ps, 64 * b + 16 * s + n + 1)
                            last = dve.tensor_reduce(mx[:, s % 2].rearrange("p t g -> p (t g)")[:, n:n + 1],
                                                     ps[:, MX_BANK + n % 2, :], AX_X, ALU.max)
                            last.then_inc(max_read, 1)
                        dve.wait_ge(max_read, 64 * b + 16 * s + 16)
                        m, r, p = mx[:, s % 2], mr[:, s % 2], mp[:, s % 2]
                        if s >= 2:
                            dve.wait_ge(mT_ps, STEPS * b + s - 1)
                        link(dve.tensor_scalar(p[:, :, 0, :], m, -1.0, None, ALU.mult))
                        link(dve.scalar_tensor_tensor(out=r, in0=m, scalar=-1.0, in1=p[:, :, 0, :],
                                                      op0=ALU.mult, op1=ALU.subtract))
                        link(dve.tensor_copy(p[:, :, 1, :], r))
                        link(dve.tensor_tensor(r, r, p[:, :, 1, :], ALU.subtract))
                        dve.tensor_copy(p[:, :, 2, :], r).then_inc(m_split, 1)

                    def attention_out():
                        dve.wait_ge(oT_ps, b + 1)
                        oT = ps[:, 4:6, :].rearrange("p k (n f) -> p (k n) f", f=P)
                        link(dve.reciprocal(rden[:], oT.rearrange("p n (g f) -> p n g f", g=G)[:, :, :, 16:18]))
                        for a in range(2):
                            for c in range(2):
                                for t in range(NT):
                                    src = oT[:, 2 * t + a, :].rearrange("p (g f) -> p g f", g=G)
                                    dst = o_nat[:, t, :].rearrange("p (g f) -> p g f", g=G)
                                    last = dve.tensor_tensor(
                                        dst[:, :, 16 * a + HD * c:16 * a + HD * c + HD],
                                        src[:, :, HD * c:HD * c + HD],
                                        rden[:, 2 * t + a, :, c].unsqueeze(2).to_broadcast([P, G, HD]), ALU.mult)
                        last.then_inc(on_ready, 1)

                    def gated(n):
                        dve.wait_ge(up_ps, NG * b + n + 1)
                        dve.wait_ge(silu_done, NG * b + n + 1)
                        if L == 1 and n >= 2 * EB and n % EB == 0:
                            dve.wait_ge(y_ps, (E + 1) * b + n // EB)
                        dst = hT[:, 0, n, :] if L == 0 else hT[:, (n // EB) % 2, n % EB, :]
                        dve.tensor_tensor(dst, ps[:, GU[n % 2][1], :], sil[:, n % 2, :], ALU.mult).then_inc(h_ready, 1)

                    b_out = b_proj[L][:].unsqueeze(1).to_broadcast([P, NT, D])
                    if L == 0:
                        gated(0)
                        attention_out()
                        for n in range(1, NG):
                            gated(n)
                        dve.wait_ge(y_ps, b + 1)
                        link(dve.tensor_tensor(x_out[:], ps[:, 7, :].rearrange("p (t d) -> p t d", d=D), x_in[:],
                                               ALU.add))
                        dve.tensor_tensor(x_out[:], x_out[:], b_out, ALU.add).then_inc(out_ready, 1)
                    else:
                        dve.wait_ge(logit_ps, b + 1)
                        lg = ps[:, MT_BANK, 0:NT * E].rearrange("p (t e) -> p t e", e=E)

                        def wide(v):
                            return v.unsqueeze(2).to_broadcast([P, NT, E])

                        link(dve.tensor_reduce(r_s[:, 0], lg, AX_X, ALU.max))
                        dve.tensor_tensor(r_t[:, 0], lg, wide(r_s[:, 0]), ALU.subtract).then_inc(lg_ready, 1)
                        dve.wait_ge(rexp_done, b + 1)
                        link(dve.tensor_reduce(r_s[:, 0], r_t[:, 1], AX_X, ALU.add))
                        link(dve.reciprocal(r_s[:, 1], r_s[:, 0]))
                        link(dve.tensor_tensor(r_p[:], r_t[:, 1], wide(r_s[:, 1]), ALU.mult))
                        for k in range(2):
                            link(dve.tensor_reduce(r_s[:, 2 + k], r_p[:], AX_X, ALU.max))
                            link(dve.tensor_tensor(r_t[:, 2], r_p[:], wide(r_s[:, 2 + k]), ALU.is_equal))
                            link(dve.scalar_tensor_tensor(out=r_t[:, 3], in0=r_t[:, 2], scalar=-99.0, in1=iota_hi[:],
                                                          op0=ALU.mult, op1=ALU.add))
                            link(dve.tensor_reduce(r_s[:, 4], r_t[:, 3], AX_X, ALU.min))
                            link(dve.tensor_tensor(oh[:, :, k, :], iota_e[:], wide(r_s[:, 4]), ALU.is_equal))
                            if k == 0:
                                link(dve.scalar_tensor_tensor(out=r_p[:], in0=oh[:, :, 0, :], scalar=-2.0, in1=r_p[:],
                                                              op0=ALU.mult, op1=ALU.add))
                        link(dve.tensor_tensor(r_s[:, 0], r_s[:, 2], r_s[:, 3], ALU.add))
                        dve.tensor_scalar(r_s[:, 1], r_s[:, 0], 1e-9, None, ALU.add).then_inc(oh_ready, 1)
                        dve.wait_ge(oh_ready, b + 1)
                        link(dve.reciprocal(r_s[:, 0], r_s[:, 1]))
                        link(dve.tensor_tensor(r_s[:, 5], r_s[:, 2], r_s[:, 0], ALU.mult))
                        link(dve.tensor_tensor(r_s[:, 6], r_s[:, 3], r_s[:, 0], ALU.mult))
                        attention_out()
                        gated(0)
                        dve.wait_ge(rank_ps, b + 1)
                        NK = 2 * E
                        link(dve.tensor_copy(tot[:].rearrange("p t k -> p (t k)"), ps[:, MT_BANK, 128:128 + NT * NK]))
                        for t in range(NT):
                            link(dve.tensor_tensor(rk[:, t, :], ps[:, MT_BANK, 64 + t * NK:64 + (t + 1) * NK],
                                                   carry[:, t % 2, :], ALU.add))
                            link(dve.tensor_tensor(carry[:, (t + 1) % 2, :], carry[:, t % 2, :], tot[:, t, :],
                                                   ALU.add))
                        rk4 = rk[:].rearrange("p t (k e) -> p t k e", e=E)
                        for k in range(2):
                            link(dve.tensor_scalar(r_t[:, 2], rk4[:, :, k, :], float(CAP), None, ALU.is_le))
                            link(dve.tensor_tensor(r_t[:, 3], r_t[:, 2], oh[:, :, k, :], ALU.mult))
                            dst = comb[:] if k == 0 else r_t[:, 0]
                            link(dve.tensor_tensor(dst, r_t[:, 3], wide(r_s[:, 5 + k]), ALU.mult))
                        link(dve.tensor_tensor(comb[:], comb[:], r_t[:, 0], ALU.add))
                        gated(1)
                        dve.wait_ge(y_ps, (E + 1) * b + 1)
                        link(dve.tensor_tensor(x_out[:], ps[:, 6, :].rearrange("p (t d) -> p t d", d=D), x_in[:],
                                               ALU.add))
                        link(dve.tensor_tensor(x_out[:], x_out[:], b_out, ALU.add))
                        for e in range(E):
                            if e + 1 < E:
                                for i in range(EB):
                                    gated((e + 1) * EB + i)
                            dve.wait_ge(y_ps, (E + 1) * b + e + 2)
                            for t in range(NT):
                                last = dve.scalar_tensor_tensor(
                                    out=x_out[:, t, :], in0=ps[:, 4 + e % 2, t * P:(t + 1) * P],
                                    scalar=comb[:, t, e:e + 1], in1=x_out[:, t, :], op0=ALU.mult, op1=ALU.add)
                            last.then_inc(y_read, 1)
                            dve.wait_ge(y_read, E * b + e + 1)
                    assert n_link[0] == CH, n_link[0]

            return sync_program, pool_program, tensor_program, scalar_program, vector_program, last_stores

        s0, p0, t0, a0, v0, stores0 = layer(0)
        s1, p1_, t1, a1, v1, stores1 = layer(1)

        @block.sync
        def _(sp):
            setup_sync(sp)
            s0(sp)
            stores0(sp)
            s1(sp)
            stores1(sp)

        @block.gpsimd
        def _(pool):
            setup_pool(pool)
            p0(pool)
            p1_(pool)

        @block.vector
        def _(dve):
            setup_vector(dve)
            v0(dve)
            v1(dve)

        @block.scalar
        def _(act):
            a0(act)
            a1(act)

        @block.tensor
        def _(pe):
            t0(pe)
            t1(pe)


def kernel(L0_attn_x, L0_attn_qkv_w, L0_attn_qkv_b, L0_attn_proj_w, L0_attn_proj_b, L0_ffn_w_gate, L0_ffn_w_up,
           L0_ffn_w_down, L1_attn_Wq, L1_attn_bq, L1_attn_Wk, L1_attn_bk, L1_attn_Wv, L1_attn_bv, L1_attn_Wo,
           L1_attn_bo, L1_attn_src_blocks, L1_attn_tgt_blocks, L1_ffn_gate_w, L1_ffn_gate_proj_w,
           L1_ffn_up_proj_w, L1_ffn_down_proj_w):
    import numpy as np
    import concourse.bacc as bacc
    from concourse.bass_utils import run_bass_kernel_spmd

    def T(a, *axes):
        return np.ascontiguousarray(np.transpose(np.asarray(a), axes or None))

    arrays = {
        "x": np.asarray(L0_attn_x),
        "qkv_wT": T(L0_attn_qkv_w), "qkv_b": np.asarray(L0_attn_qkv_b),
        "proj_wT": T(L0_attn_proj_w), "proj_b": np.asarray(L0_attn_proj_b),
        "wg_T": T(L0_ffn_w_gate), "wu_T": T(L0_ffn_w_up), "wd_T": T(L0_ffn_w_down),
        "Wq_T": T(L1_attn_Wq), "bq": np.asarray(L1_attn_bq),
        "Wk_T": T(L1_attn_Wk), "bk": np.asarray(L1_attn_bk),
        "Wv_T": T(L1_attn_Wv), "bv": np.asarray(L1_attn_bv),
        "Wo_T": T(L1_attn_Wo), "bo": np.asarray(L1_attn_bo),
        "src_blocks": np.asarray(L1_attn_src_blocks), "tgt_blocks": np.asarray(L1_attn_tgt_blocks),
        "router_T": T(L1_ffn_gate_w),
        "eg_T": T(L1_ffn_gate_proj_w, 2, 0, 1), "eu_T": T(L1_ffn_up_proj_w, 2, 0, 1),
        "ed_T": T(L1_ffn_down_proj_w, 0, 2, 1),
    }
    nc = bacc.Bacc("TRN2", target_bir_lowering=False, num_devices=1)
    args = {n: nc.dram_tensor("in_" + n, a.shape, mybir.dt.from_np(a.dtype), kind="ExternalInput").ap()
            for n, a in arrays.items()}
    out = nc.dram_tensor("out_y", arrays["x"].shape, F32, kind="ExternalOutput").ap()
    build(nc, out=out, **args)
    r = run_bass_kernel_spmd(nc, [{"in_" + n: a for n, a in arrays.items()}], core_ids=[0])
    return r.results[0]["out_y"]
```

```python
from contextlib import ExitStack

import concourse.bass as bass
from concourse import mybir

F32 = mybir.dt.float32
BF16 = mybir.dt.bfloat16
I32 = mybir.dt.int32
ALU = mybir.AluOpType
ACT = mybir.ActivationFunctionType
AX_X = mybir.AxisListType.X

P = 128
EPS = 1e-5
MASKED = -1e30


def build(nc, x, qkv_wT, qkv_b, proj_wT, proj_b, wg_T, wu_T, wd_T, Wq_T, bq, Wk_T, bk, Wv_T, bv, Wo_T, bo,
          src_blocks, tgt_blocks, router_T, eg_T, eu_T, ed_T, out):
    B, S, D = x.shape
    H, HD = 16, 8
    NT = S // P
    G = 4
    STEPS = H // G
    HID = wg_T.shape[1]
    HB = HID // P
    E, EH = eg_T.shape[1], eg_T.shape[2]
    EB = EH // P
    T = B * S
    CAP = int(1.25 * T / E)
    NB = S // 64
    SLOT = 64
    ROWS = 96
    M_ROW, MASK_ROW = 48, 64
    QSCALE = HD ** -0.5
    NSRC = src_blocks.shape[0]

    x_mid = nc.dram_tensor("x_mid", (B, S, D), F32, kind="Internal").ap()
    v_bounce = nc.dram_tensor("v_bounce", (S, D), F32, kind="Internal").ap()

    with ExitStack() as ctx:
        def sb(name, shape, dt=F32):
            return ctx.enter_context(nc.sbuf_tensor(name, shape, dt))

        def sem(name):
            return ctx.enter_context(nc.semaphore(name))

        ident = sb("ident", [P, P])
        ident_bf = sb("ident_bf", [P, P], BF16)
        zero_f = sb("zero_f", [P, S])
        tri = sb("tri", [P, P], BF16)
        ones_bf = sb("ones_bf", [P, P], BF16)
        w_qkv = [sb("w_qkv0", [P, 3 * D]), sb("w_qkv1", [P, 3 * D])]
        b_qkv = [sb("b_qkv0", [P, 3 * D]), sb("b_qkv1", [P, 3 * D])]
        w_proj = [sb("w_proj0", [P, D]), sb("w_proj1", [P, D])]
        b_proj = [sb("b_proj0", [P, D]), sb("b_proj1", [P, D])]
        wg_i = sb("wg_i", [P, HID], I32)
        wu_i = sb("wu_i", [P, HID], I32)
        wd_i = sb("wd_i", [P, HB, D], I32)
        wg = sb("wg", [P, HID])
        wu = sb("wu", [P, HID])
        wd = sb("wd", [P, HB, D])
        w_router = sb("w_router", [P, E])
        eg = sb("eg", [P, E, EH])
        eu = sb("eu", [P, E, EH])
        ed = sb("ed", [P, E, EB, D])
        st_i = sb("st_i", [NB, 2, NSRC], I32)
        st_f = sb("st_f", [NB, 2, NSRC])
        blk_q = sb("blk_q", [NB, NB])
        blk_k = sb("blk_k", [NB, NB])
        hits = sb("hits", [NB, NB])
        tmp8 = sb("tmp8", [NB, 4, NB])
        mask_q = sb("mask_q", [NB, S], BF16)
        onehot_k = sb("onehot_k", [NB, S], BF16)
        x_next = sb("x_next", [P, NT, D])
        xnT_next = sb("xnT_next", [P, S])
        x_in = sb("x_in", [P, NT, D])
        x_out = sb("x_out", [P, NT, D])
        stats = sb("stats", [P, NT, 6])
        mv = sb("mv", [P, NT, 2])
        rstd = sb("rstd", [P, NT])
        var_eps = sb("var_eps", [P, NT])
        eps_t = sb("eps_t", [P, NT])
        neg_half = sb("neg_half", [P, NT])
        wait_taker = sb("wait_taker", [P, NT])
        pool_taker = sb("pool_taker", [P, 5, NT])
        xn = sb("xn", [P, NT, D])
        xnT = sb("xnT", [P, S])
        qk = sb("qk", [P, 2, NT, D])
        part = [sb(f"part{i}", [P, 2, NT * H, HD], BF16) for i in range(3)]
        rest = [sb(f"rest{i}", [P, 2, NT, D]) for i in range(2)]
        v_nat = sb("v_nat", [P, NT, D])
        Rq = sb("Rq", [P, NT * H, SLOT], BF16)
        Rk = sb("Rk", [P, NT * H, SLOT], BF16)
        QO = sb("QO", [ROWS, H, S], BF16)
        KO = sb("KO", [ROWS, H, S], BF16)
        Vp = sb("Vp", [P, NT, H, 32])
        PT = sb("PT", [P, 4, 2, S])
        mx = sb("mx", [P, 2, NT, G])
        mr = sb("mr", [P, 2, NT, G])
        mp = sb("mp", [P, 2, NT, 3, G], BF16)
        mT = sb("mT", [3 * G, 2, S], BF16)
        o_sb = sb("o_sb", [P, 2, S])
        rden = sb("rden", [P, NT * 2, G, 2])
        o_nat = sb("o_nat", [P, NT, D])
        o_T = sb("o_T", [P, S])
        sil = sb("sil", [P, 2, S])
        hT = sb("hT", [P, 2, max(HB, EB), S])
        iota_e = sb("iota_e", [P, NT, E])
        iota_hi = sb("iota_hi", [P, NT, E])
        r_p = sb("r_p", [P, NT, E])
        r_t = sb("r_t", [P, 4, NT, E])
        r_s = sb("r_s", [P, 8, NT])
        oh = sb("oh", [P, NT, 2, E], BF16)
        rk = sb("rk", [P, NT, 2 * E])
        tot = sb("tot", [P, NT, 2 * E])
        carry = sb("carry", [P, 2, 2 * E])
        comb = sb("comb", [P, NT, E])

        ps = ctx.enter_context(nc.psum_tensor("ps", [P, 8, 512], F32))

        def ps_bf(bank):
            return ps[:, bank, :].bitcast(BF16)

        MX_BANK, PV_BANK, SIDE_BANK = 4, 6, 7
        ROUTER_BANK, Q_BANK, K_BANK = 3, 6, 7

        loaded = sem("loaded")
        first_loaded = sem("first_loaded")
        first_ready = sem("first_ready")
        consts = sem("consts")
        cleared = sem("cleared")
        dve_setup = sem("dve_setup")
        ready = sem("ready")
        rows_in = sem("rows_in")
        key_rows_in = sem("key_rows_in")
        mask_ready = sem("mask_ready")

        first_loads = [(w_qkv[0][:], qkv_wT), (b_qkv[0][:], qkv_b[None, :].to_broadcast([P, 3 * D]))]
        loads = [(w_proj[0][:], proj_wT), (b_proj[0][:], proj_b[None, :].to_broadcast([P, D])),
                 (wg_i[:], wg_T), (wu_i[:], wu_T), (wd_i[:], wd_T.rearrange("(b p) d -> p b d", p=P)),
                 (w_proj[1][:], Wo_T), (b_proj[1][:], bo[None, :].to_broadcast([P, D])),
                 (w_router[:], router_T), (eg[:], eg_T), (eu[:], eu_T),
                 (ed[:], ed_T.rearrange("e (b p) d -> p e b d", p=P)),
                 (st_i[:, 0, :], src_blocks[None, :].to_broadcast([NB, NSRC])),
                 (st_i[:, 1, :], tgt_blocks[None, :].to_broadcast([NB, NSRC]))]
        for i, (w, b) in enumerate(((Wq_T, bq), (Wk_T, bk), (Wv_T, bv))):
            loads.append((w_qkv[1][:, i * D:(i + 1) * D], w))
            loads.append((b_qkv[1][:, i * D:(i + 1) * D], b[None, :].to_broadcast([P, D])))
        N_LOAD = 16 * len(loads)
        N_FIRST = 16 * len(first_loads)

        def first_setup_sync(sp):
            for dst, src in first_loads:
                sp.dma_start(dst, src).then_inc(first_loaded, 16)

        def setup_sync(sp):
            for dst, src in loads:
                sp.dma_start(dst, src).then_inc(loaded, 16)

        def setup_pool(pool):
            for n, t in enumerate((ident, ident_bf)):
                pool.memset(t[:], 0.0).then_inc(consts, 1)
                pool.wait_ge(consts, 2 * n + 1)
                pool.affine_select(out=t[:], in_=t[:], compare_op=ALU.not_equal, fill=1.0, base=0,
                                   pattern=[[-1, P]], channel_multiplier=1).then_inc(consts, 1)
            pool.memset(tri[:], 1.0).then_inc(consts, 1)
            pool.wait_ge(consts, 5)
            pool.affine_select(out=tri[:], in_=tri[:], compare_op=ALU.is_ge, fill=0.0, base=0,
                               pattern=[[1, P]], channel_multiplier=-1).then_inc(consts, 1)
            pool.memset(ones_bf[:], 1.0).then_inc(consts, 1)
            pool.iota(iota_e[:], pattern=[[0, NT], [1, E]], base=0, channel_multiplier=0,
                      allow_small_or_imprecise_dtypes=True).then_inc(consts, 1)
            pool.iota(iota_hi[:], pattern=[[0, NT], [1, E]], base=99, channel_multiplier=0,
                      allow_small_or_imprecise_dtypes=True).then_inc(consts, 1)
            pool.iota(blk_q[:], pattern=[[1, NB]], base=0, channel_multiplier=0,
                      allow_small_or_imprecise_dtypes=True).then_inc(consts, 1)
            pool.iota(blk_k[:], pattern=[[0, NB]], base=0, channel_multiplier=1,
                      allow_small_or_imprecise_dtypes=True).then_inc(consts, 1)
            pool.memset(onehot_k[:], 1.0).then_inc(consts, 1)
            pool.wait_ge(consts, 12)
            pool.affine_select(out=onehot_k[:], in_=onehot_k[:], compare_op=ALU.is_ge, fill=0.0, base=0,
                               pattern=[[1, S]], channel_multiplier=-64).then_inc(consts, 1)
            pool.wait_ge(consts, 13)
            pool.affine_select(out=onehot_k[:], in_=onehot_k[:], compare_op=ALU.is_ge, fill=0.0, base=63,
                               pattern=[[-1, S]], channel_multiplier=64).then_inc(consts, 1)
            pool.memset(zero_f[:], 0.0)
            pool.memset(eps_t[:], EPS)
            pool.memset(neg_half[:], -0.5)
            pool.memset(Rk[:], 0.0).then_inc(cleared, 1)
            pool.memset(Rq[:], 0.0).then_inc(cleared, 1)
            pool.wait_ge(cleared, 2)
            pool.memset(Rk[:, :, M_ROW:M_ROW + 3], 1.0).then_inc(cleared, 1)
            pool.memset(Vp[:], 0.0).then_inc(cleared, 1)
            pool.wait_ge(cleared, 4)
            for c in range(2):
                pool.memset(Vp[:, :, c:H:2, 16 + c:17 + c], 1.0).then_inc(cleared, 1)
            pool.wait_ge(cleared, N_CLEARED)

        N_CONST, N_CLEARED = 14, 6

        def scale_q(dve, layer):
            dve.tensor_scalar(w_qkv[layer][:, 0:D], w_qkv[layer][:, 0:D], QSCALE, None, ALU.mult)
            return dve.tensor_scalar(b_qkv[layer][:, 0:D], b_qkv[layer][:, 0:D], QSCALE, None, ALU.mult)

        def first_setup_vector(dve):
            dve.memset(QO[64:96], 0.0)
            dve.memset(KO[64:96], 0.0)
            dve.wait_ge(first_loaded, N_FIRST)
            scale_q(dve, 0).then_inc(first_ready, 1)
            dve.wait_ge(first_ready, 1)
            dve.wait_ge(cleared, N_CLEARED)

        def setup_vector(dve):
            n = [0]

            def link(ins):
                n[0] += 1
                ins.then_inc(dve_setup, 1)
                dve.wait_ge(dve_setup, n[0])

            dve.memset(carry[:], 0.0).then_inc(dve_setup, 1)
            n[0] += 1
            dve.wait_ge(loaded, N_LOAD)
            for i, f, w in ((wg_i, wg, None), (wu_i, wu, None), (wd_i, wd, None)):
                link(dve.tensor_copy(f[:], i[:]))
                dve.tensor_scalar(f[:], f[:], 1.0 / 127.0, None, ALU.mult)
            scale_q(dve, 1)
            link(dve.tensor_copy(st_f[:], st_i[:]))
            dve.wait_ge(consts, N_CONST)
            link(dve.tensor_tensor(tmp8[:, 0, :], blk_q[:], blk_k[:], ALU.subtract))
            link(dve.tensor_tensor(tmp8[:, 1, :], tmp8[:, 0, :], tmp8[:, 0, :], ALU.mult))
            link(dve.tensor_scalar(hits[:], tmp8[:, 1, :], 1.0, None, ALU.is_le))
            for j in (0, NB - 1):
                link(dve.tensor_scalar(tmp8[:, 0, :], blk_k[:], float(j), None, ALU.is_equal))
                link(dve.tensor_tensor(hits[:], hits[:], tmp8[:, 0, :], ALU.add))
            for n_pair in range(NSRC):
                for side, blk in ((0, blk_q), (1, blk_k)):
                    v = st_f[:, side, n_pair:n_pair + 1]
                    link(dve.tensor_scalar(tmp8[:, 2, :], blk[:], v, None, ALU.is_equal))
                    link(dve.tensor_scalar(tmp8[:, 3, :], blk[:], float(NB), v, ALU.subtract, ALU.is_equal))
                    link(dve.tensor_tensor(tmp8[:, side, :], tmp8[:, 2, :], tmp8[:, 3, :], ALU.add))
                link(dve.tensor_tensor(tmp8[:, 0, :], tmp8[:, 0, :], tmp8[:, 1, :], ALU.mult))
                link(dve.tensor_tensor(hits[:], hits[:], tmp8[:, 0, :], ALU.add))
            link(dve.tensor_scalar(hits[:], hits[:], 0.5, MASKED, ALU.is_lt, ALU.mult))
            dve.tensor_copy(mask_q[:].rearrange("p (b t) -> p b t", b=NB),
                            hits[:].unsqueeze(2).to_broadcast([NB, NB, 64])).then_inc(mask_ready, 1)
            dve.tensor_copy(tmp8[:, 0, :], blk_q[:]).then_inc(ready, 1)

        x_loaded = sem("x_loaded")
        x_taken = sem("x_taken")
        stats_done = sem("stats_done")
        mv_ready = sem("mv_ready")
        rstd_ready = sem("rstd_ready")
        xn_ready = sem("xn_ready")
        xnT_ps = sem("xnT_ps")
        xnT_ready = sem("xnT_ready")
        qkv_ps = sem("qkv_ps")
        qkv_read = sem("qkv_read")
        v_stored = sem("v_stored")
        v_loaded = sem("v_loaded")
        v_placed = sem("v_placed")
        p1_ready = sem("p1_ready")
        p2_ready = sem("p2_ready")
        p3_ready = sem("p3_ready")
        r1_ready = sem("r1_ready")
        r2_ready = sem("r2_ready")
        R_ready = sem("R_ready")
        q_ps = sem("q_ps")
        k_ps = sem("k_ps")
        q_copied = sem("q_copied")
        k_copied = sem("k_copied")
        max_ps = sem("max_ps")
        max_read = sem("max_read")
        m_chain = sem("m_chain")
        m_split = sem("m_split")
        mT_ps = sem("mT_ps")
        mT_ready = sem("mT_ready")
        m_rows = sem("m_rows")
        st_ps = sem("st_ps")
        exp_done = sem("exp_done")
        pv_done = sem("pv_done")
        o_copied = sem("o_copied")
        oT_ps = sem("oT_ps")
        rden_ready = sem("rden_ready")
        on_ready = sem("on_ready")
        onT_ps = sem("onT_ps")
        onT_ready = sem("onT_ready")
        unit_done = sem("unit_done")
        stored = sem("stored")
        gate_ps = [sem(f"gate_ps{i}") for i in range(2)]
        up_ps = [sem(f"up_ps{i}") for i in range(2)]
        silu_done = [sem(f"silu_done{i}") for i in range(2)]
        h_ready = [sem(f"h_ready{i}") for i in range(2)]
        y_ps = [sem(f"y_ps{i}") for i in range(2)]
        out_chain = [sem(f"out_chain{i}") for i in range(2)]
        logit_ps = sem("logit_ps")
        lg_ready = sem("lg_ready")
        rexp_done = sem("rexp_done")
        oh_ready = sem("oh_ready")
        rank_ps = sem("rank_ps")
        route_chain = sem("route_chain")
        y_read = sem("y_read")

        EXPS = 2 * NT
        M_DMAS = 3
        MAXES = NT * G

        def head(s, g):
            return 4 * g + s

        def gate_ups(L):
            return HB if L == 0 else E * EB

        def gate_up_weights(L, n):
            if L == 0:
                return wg[:, n * P:(n + 1) * P], wu[:, n * P:(n + 1) * P]
            e, i = n // EB, n % EB
            return eg[:, e, i * P:(i + 1) * P], eu[:, e, i * P:(i + 1) * P]

        def gu_bank(m):
            return m % 3

        class Unit:

            def __init__(self, L, b):
                self.L, self.b, self.u = L, b, B * L + b

        def load_x(sp, n):
            if n.L == 1:
                sp.wait_ge(stored, 16 * n.b + 32)
            src = (x if n.L == 0 else x_mid)[n.b]
            sp.dma_start(x_next[:], src.rearrange("(t p) d -> p t d", p=P)).then_inc(x_loaded, 16)

        def max_rows_in(sp, w, s):
            sp.wait_ge(mT_ready, STEPS * w.u + s + 1)
            for i in range(3):
                sp.dma_start(QO[M_ROW + i:M_ROW + i + 1, s:H:G, :],
                             mT[G * i:G * i + G, s % 2, :]).then_inc(m_rows, 16)

        def place_values_1(sp, n):
            sp.wait_ge(pv_done, NT * STEPS * n.u)
            sp.wait_ge(qkv_read, NT * n.u + NT)
            sp.dma_start(v_bounce.rearrange("(t p) d -> p t d", p=P), v_nat[:]).then_inc(v_stored, 16)
            sp.wait_ge(v_stored, 16 * n.b + 16)
            v_pos = v_bounce.rearrange("(h k t) (c d) -> k (t c) h d", h=H, k=NT, c=H)
            for k in range(NT):
                for c in range(2):
                    sp.dma_start(Vp[:, k, c:H:2, HD * c:HD * c + HD], v_pos[k][:, c:H:2, :]).then_inc(v_loaded, 16)

        def store_x(sp, w):
            sp.wait_ge(unit_done, w.u + 2)
            dst = (x_mid if w.L == 0 else out)[w.b]
            sp.dma_start(dst.rearrange("(t p) d -> p t d", p=P), x_out[:]).then_inc(stored, 16)

        def sync_unit(sp, w, n):
            if n is not None:
                sp.wait_ge(x_taken, 2 * w.u + 2)
                load_x(sp, n)
            for s in range(STEPS):
                max_rows_in(sp, w, s)
            if n is not None and n.L == 1:
                place_values_1(sp, n)
            store_x(sp, w)

        def reciprocal_deviation(pool, n):
            pool.wait_ge(mv_ready, n.u + 1)
            pool.tensor_tensor(var_eps[:], mv[:, :, 1], eps_t[:], ALU.add).then_inc(rstd_ready, 1)
            pool.wait_ge(rstd_ready, 2 * n.u + 1)
            pool.tensor_tensor(rstd[:], var_eps[:], neg_half[:], ALU.pow).then_inc(rstd_ready, 1)

        def take_x(pool, w):
            pool.wait_ge(unit_done, w.u + 1)
            pool.tensor_tensor(pool_taker[:, 0], eps_t[:], eps_t[:], ALU.add)
            pool.tensor_copy(x_in[:], x_next[:]).then_inc(x_taken, 1)
            pool.tensor_copy(xnT[:], xnT_next[:]).then_inc(x_taken, 1)

        def fill_slots(pool, n):
            Rs = [R[:, :, 0:48].rearrange("p n (s d) -> p n s d", d=HD) for R in (Rq, Rk)]
            slots = [((0, 3, 1), (2, 5, 1)), ((3, 6, 2), (1, 6, 4)), ((4, 5, 1), (0, 1, 1))]
            for i, done in enumerate((p1_ready, p2_ready, p3_ready)):
                pool.wait_ge(done, n.u + 1)
                pool.tensor_tensor(pool_taker[:, 1 + i], eps_t[:], eps_t[:], ALU.add)
                for side in range(2):
                    a, z, step = slots[i][side]
                    count = len(range(a, z, step))
                    pool.tensor_copy(Rs[side][:, :, a:z:step, :],
                                     part[i][:, side].unsqueeze(2).to_broadcast([P, NT * H, count, HD])
                                     ).then_inc(R_ready, 1)

        def place_values_0(pool, n):
            if n is not FIRST:
                pool.wait_ge(pv_done, NT * STEPS * n.u)
                pool.tensor_tensor(pool_taker[:, 4], eps_t[:], eps_t[:], ALU.add)
            for c in range(2):
                src = v_nat[:].rearrange("p t (h c d) -> p c t h d", c=2, d=HD)[:, c]
                pool.tensor_copy(Vp[:, :, c:H:2, HD * c:HD * c + HD], src).then_inc(v_placed, 1)

        def pool_unit(pool, w, n):
            take_x(pool, w)
            if n is not None:
                reciprocal_deviation(pool, n)
                fill_slots(pool, n)
                if n.L == 0:
                    place_values_0(pool, n)

        def xnT_mms(pe, n):
            pe.wait_ge(xn_ready, n.u + 1)
            for t in range(NT):
                last = pe.transpose(ps[:, SIDE_BANK, t * P:(t + 1) * P], xn[:, t, :], ident[:])
            last.then_inc(xnT_ps, 1)

        def qkv_mm(pe, n, t):
            if t == 0:
                pe.wait_ge(xnT_ready, n.u + 1)
            else:
                pe.wait_ge(qkv_read, NT * n.u + t)
            pe.matmul(ps[:, SIDE_BANK, 0:3 * D], xnT_next[:, t * P:(t + 1) * P], w_qkv[n.L][:],
                      start=True, stop=True).then_inc(qkv_ps, 1)

        def operand_transposes(pe, n, side, j):
            ps_done, copied, R, bank = ((q_ps, q_copied, Rq, Q_BANK), (k_ps, k_copied, Rk, K_BANK))[side]
            if j == 0 and side == 0:
                pe.wait_ge(R_ready, 6 * n.u + 6)
            if j > 0:
                pe.wait_ge(copied, 8 * n.u + 2 * j)
            Rv = R[:].rearrange("p (t h) s -> p t (h s)", t=NT)
            for a in range(2):
                for t in range(NT):
                    c0 = (2 * j + a) * 2 * SLOT
                    last = pe.transpose(ps_bf(bank)[:, a * S + t * P:a * S + (t + 1) * P],
                                        Rv[:, t, c0:c0 + 2 * SLOT], ident_bf[:])
            last.then_inc(ps_done, 1)

        def max_mm(pe, w, s, i):
            qt, g = i // G, i % G
            if s == 0 and i == 0:
                pe.wait_ge(q_copied, 8 * w.u + 8)
                pe.wait_ge(k_copied, 8 * w.u + 8)
            if s > 0 or i >= 2:
                pe.wait_ge(max_read, MAXES * (STEPS * w.u + s) + i - 1)
            h = head(s, g)
            pe.matmul(ps[:, MX_BANK + i % 2, :], QO[:, h, qt * P:(qt + 1) * P], KO[:, h, :],
                      start=True, stop=True).then_inc(max_ps, 1)

        def max_transposes(pe, w, s):
            pe.wait_ge(m_split, STEPS * w.u + s + 1)
            for t in range(NT):
                last = pe.transpose(ps_bf(SIDE_BANK)[0:3 * G, t * P:(t + 1) * P],
                                    mp[:, s % 2, t].rearrange("p i g -> p (i g)"), ident_bf[:])
            last.then_inc(mT_ps, 1)

        def score_mm(pe, w, s, k, g):
            i = 2 * k + g // 2
            if g % 2 == 0 and (s > 0 or i >= 2):
                pe.wait_ge(exp_done, EXPS * (STEPS * w.u + s) + i - 1)
            h = head(s, g)
            mm = pe.matmul(ps[:, 2 * (i % 2) + g % 2, :], KO[:, h, k * P:(k + 1) * P], QO[:, h, :],
                           start=True, stop=True)
            if g % 2 == 1:
                mm.then_inc(st_ps, 1)

        def value_mms(pe, w, s, k):
            pe.wait_ge(exp_done, EXPS * (STEPS * w.u + s) + 2 * k + 2)
            if s == 2 and k == 0:
                pe.wait_ge(o_copied, 2 * w.u + 1)
            if s == 0 and k == 0:
                if w.L == 0:
                    pe.wait_ge(v_placed, 2 * w.u + 2)
                else:
                    pe.wait_ge(v_loaded, 128 * w.b + 128)
            for g in range(G):
                last = pe.matmul(ps[32 * g:32 * g + 32, PV_BANK, :], Vp[:, k, head(s, g), :],
                                 PT[:, (2 * k + g // 2) % 4, g % 2, :],
                                 start=(s % 2 == 0 and k == 0), stop=(s % 2 == 1 and k == NT - 1))
            last.then_inc(pv_done, 1)

        def gate_up(pe, w, i):
            L, NG = w.L, gate_ups(w.L)
            for m, weight, done in ((2 * i, gate_up_weights(L, i)[0], gate_ps), (2 * i + 1, gate_up_weights(L, i)[1], up_ps)):
                before = m - 3
                if before >= 0:
                    pe.wait_ge((h_ready if before % 2 else silu_done)[L], NG * w.b + before // 2 + 1)
                pe.matmul(ps[:, gu_bank(m), :], weight, xnT[:], start=True, stop=True).then_inc(done[L], 1)

        def out_transposes(pe, w):
            pe.wait_ge(o_copied, 2 * w.u + 2)
            for t in range(NT):
                for a in range(2):
                    c0 = ((t % 2) * 2 + a) * P
                    last = pe.transpose(ps[:, 4 + t // 2, c0:c0 + P], o_sb[:, a, t * P:(t + 1) * P], ident[:])
            last.then_inc(oT_ps, 1)

        def normalized_transposes(pe, w):
            pe.wait_ge(on_ready, w.u + 1)
            for t in range(NT):
                last = pe.transpose(ps[:, 4, t * P:(t + 1) * P], o_nat[:, t, :], ident[:])
            last.then_inc(onT_ps, 1)

        def out_mms_0(pe, w):
            pe.wait_ge(onT_ready, w.u + 1)
            pe.wait_ge(h_ready[0], HB * w.b + HB)
            for t in range(NT):
                tok = slice(t * P, (t + 1) * P)
                pe.matmul(ps[:, 5, tok], o_T[:, tok], w_proj[0][:], start=True, stop=False)
                for i in range(HB):
                    last = pe.matmul(ps[:, 5, tok], hT[:, 0, i, tok], wd[:, i, :], start=False, stop=(i == HB - 1))
            last.then_inc(y_ps[0], 1)

        def out_mms_1(pe, w):
            pe.wait_ge(onT_ready, w.u + 1)
            for t in range(NT):
                tok = slice(t * P, (t + 1) * P)
                last = pe.matmul(ps[:, 5, tok], o_T[:, tok], w_proj[1][:], start=True, stop=True)
            last.then_inc(y_ps[1], 1)

        def router_mms(pe, w):
            for t in range(NT):
                last = pe.matmul(ps[:, ROUTER_BANK, t * E:(t + 1) * E], xnT[:, t * P:(t + 1) * P], w_router[:],
                                 start=True, stop=True)
            last.then_inc(logit_ps, 1)

        def rank_mms(pe, w):
            pe.wait_ge(oh_ready, w.b + 1)
            oh2 = oh[:].rearrange("p t k e -> p (t k e)")
            n_oh = NT * 2 * E
            pe.matmul(ps[:, ROUTER_BANK, 64:64 + n_oh], tri[:], oh2, start=True, stop=True)
            pe.matmul(ps[:, ROUTER_BANK, 128:128 + n_oh], ones_bf[:], oh2,
                      start=True, stop=True).then_inc(rank_ps, 1)

        def expert_out(pe, w, e):
            pe.wait_ge(h_ready[1], E * EB * w.b + (e + 1) * EB)
            if e >= 1:
                pe.wait_ge(y_read, (E + 1) * w.b + e)
            for t in range(NT):
                tok = slice(t * P, (t + 1) * P)
                for i in range(EB):
                    last = pe.matmul(ps[:, 4 + e % 2, tok], hT[:, e % 2, i, tok], ed[:, e, i, :],
                                     start=(i == 0), stop=(i == EB - 1))
            last.then_inc(y_ps[1], 1)

        def side_mms(pe, w, n, s, k):
            if k == 1 and s + 1 < STEPS:
                if n is not None and s >= 1:
                    pe.wait_ge(qkv_read, NT * n.u + (1 if s == 1 else NT))
                max_transposes(pe, w, s + 1)
            if n is not None:
                if (s, k) == (0, 2):
                    pe.wait_ge(mT_ready, STEPS * w.u + 2)
                    xnT_mms(pe, n)
                tiles = {(1, 0): 0, (1, 2): 1, (1, 3): 2, (2, 0): 3}
                if (s, k) in tiles:
                    if (s, k) == (1, 2):
                        pe.wait_ge(mT_ready, STEPS * w.u + 3)
                    qkv_mm(pe, n, tiles[s, k])

        def tensor_unit(pe, w, n):
            pe.wait_ge(unit_done, w.u + 1)
            for i in range(MAXES):
                max_mm(pe, w, 0, i)
            for i in range(MAXES):
                max_mm(pe, w, 1, i)
                if i == 7:
                    max_transposes(pe, w, 0)
            for s in range(STEPS):
                pe.wait_ge(m_rows, 16 * M_DMAS * (STEPS * w.u + s + 1))
                for k in range(NT):
                    if s == 0 and k == 1:
                        pe.wait_ge(mT_ready, STEPS * w.u + 1)
                    for g in range(G):
                        if s + 2 < STEPS:
                            max_mm(pe, w, s + 2, G * k + g)
                        score_mm(pe, w, s, k, g)
                    side_mms(pe, w, n, s, k)
                    if k > 0:
                        value_mms(pe, w, s, k - 1)
                value_mms(pe, w, s, NT - 1)

            def operands(j):
                if n is not None:
                    for side in range(2):
                        operand_transposes(pe, n, side, j)

            pe.wait_ge(x_taken, 2 * w.u + 2)
            if w.L == 0:
                gate_up(pe, w, 0)
                out_transposes(pe, w)
                for i in range(1, HB):
                    operands(i - 1)
                    gate_up(pe, w, i)
                normalized_transposes(pe, w)
                operands(HB - 1)
                out_mms_0(pe, w)
                operands(HB)
            else:
                router_mms(pe, w)
                gate_up(pe, w, 0)
                out_transposes(pe, w)
                gate_up(pe, w, 1)
                rank_mms(pe, w)
                normalized_transposes(pe, w)
                out_mms_1(pe, w)
                for e in range(E):
                    if e + 1 < E:
                        for i in range(EB):
                            gate_up(pe, w, (e + 1) * EB + i)
                    if e < 4:
                        operands(e)
                    expert_out(pe, w, e)

        def xnT_copy(act, n):
            act.wait_ge(xnT_ps, n.u + 1)
            act.copy(xnT_next[:], ps[:, SIDE_BANK, :]).then_inc(xnT_ready, 1)

        def cast_part(act, n, i):
            src = (qk, rest[0], rest[1])[i]
            if i == 0:
                act.wait_ge(qkv_read, NT * n.u + NT)
            else:
                act.wait_ge((r1_ready, r2_ready)[i - 1], n.u + 1)
            act.copy(part[i][:].rearrange("p q n d -> p (q n d)"),
                     src[:].rearrange("p q t d -> p (q t d)")).then_inc((p1_ready, p2_ready, p3_ready)[i], 1)

        def operand_copies(copy, wait, n, side, j):
            ps_done, copied, buf, bank = ((q_ps, q_copied, QO, Q_BANK), (k_ps, k_copied, KO, K_BANK))[side]
            wait(ps_done, 4 * n.u + j + 1)
            for r in range(2):
                src = ps_bf(bank)[SLOT * r:SLOT * r + SLOT, :].rearrange("p (a n) -> p a n", a=2)
                c0 = 4 * j + r
                if n.L == 0:
                    dst = buf[0:SLOT, c0:c0 + 3:2, :]
                else:
                    dst = buf[0:SLOT].rearrange("p h (t c) -> p c (h t)", c=H)[:, c0:c0 + 3:2, :]
                copy(dst, src).then_inc(copied, 1)

        def maxima_copy(act, w, s):
            act.wait_ge(mT_ps, STEPS * w.u + s + 1)
            act.copy(mT[:, s % 2, :], ps_bf(SIDE_BANK)[0:3 * G, 0:S]).then_inc(mT_ready, 1)

        def exponential(act, w, s, i):
            act.wait_ge(st_ps, EXPS * (STEPS * w.u + s) + i + 1)
            if s > 0 or i >= 4:
                act.wait_ge(pv_done, NT * (STEPS * w.u + s) + i // 2 - 1)
            act.activation(PT[:, i % 4], ps[:, 2 * (i % 2):2 * (i % 2) + 2, :], ACT.Exp).then_inc(exp_done, 1)

        def output_copy(act, w, a):
            act.wait_ge(pv_done, NT * (STEPS * w.u + 2 * a + 2))
            act.copy(o_sb[:, a, :], ps[:, PV_BANK, :]).then_inc(o_copied, 1)

        def silu(act, w, i):
            L, NG = w.L, gate_ups(w.L)
            act.wait_ge(gate_ps[L], NG * w.b + i + 1)
            if i >= 2:
                act.wait_ge(h_ready[L], NG * w.b + i - 1)
            act.activation(sil[:, i % 2, :], ps[:, gu_bank(2 * i), :], ACT.Silu).then_inc(silu_done[L], 1)

        def onT_copy(act, w):
            act.wait_ge(onT_ps, w.u + 1)
            act.copy(o_T[:], ps[:, 4, :]).then_inc(onT_ready, 1)

        def scalar_unit(act, w, n):
            maxima_copy(act, w, 0)
            for s in range(STEPS):
                for i in range(EXPS):
                    exponential(act, w, s, i)
                    if i == 3 and s + 1 < STEPS:
                        maxima_copy(act, w, s + 1)
                    if n is not None:
                        if (s, i) == (0, 5):
                            xnT_copy(act, n)
                        if (s, i) in ((2, 3), (2, 7), (3, 3)):
                            cast_part(act, n, {(2, 3): 0, (2, 7): 1, (3, 3): 2}[s, i])
                if s % 2 == 1:
                    output_copy(act, w, s // 2)

            def operands(j):
                if n is not None:
                    operand_copies(act.copy, act.wait_ge, n, 0, j)

            if w.L == 0:
                silu(act, w, 0)
                for i in range(1, HB):
                    operands(i - 1)
                    silu(act, w, i)
                onT_copy(act, w)
                operands(HB - 1)
                operands(HB)
            else:
                act.wait_ge(lg_ready, w.b + 1)
                act.activation(r_t[:, 1], r_t[:, 0], ACT.Exp).then_inc(rexp_done, 1)
                silu(act, w, 0)
                silu(act, w, 1)
                onT_copy(act, w)
                for e in range(E):
                    if e + 1 < E:
                        for i in range(EB):
                            silu(act, w, (e + 1) * EB + i)
                    if e < 4:
                        operands(e)

        def normalize(dve, n):
            dve.wait_ge(x_loaded, 16 * n.u + 16)
            for t in range(NT):
                last = dve.bn_stats(stats[:, t, :], x_next[:, t, :])
            last.then_inc(stats_done, 1)
            dve.wait_ge(stats_done, n.u + 1)
            dve.tensor_copy(wait_taker[:], eps_t[:])
            for t in range(NT):
                last = dve.bn_aggr(mv[:, t, :], stats[:, t, :])
            last.then_inc(mv_ready, 1)
            dve.wait_ge(rstd_ready, 2 * n.u + 2)
            for t in range(NT):
                last = dve.tensor_scalar(xn[:, t, :], x_next[:, t, :], mv[:, t, 0:1], rstd[:, t:t + 1],
                                         ALU.subtract, ALU.mult)
            last.then_inc(xn_ready, 1)

        def read_qkv(dve, n, t):
            dve.wait_ge(qkv_ps, NT * n.u + t + 1)
            bias = b_qkv[n.L]
            dve.tensor_tensor(qk[:, :, t, :], ps[:, SIDE_BANK, 0:2 * D].rearrange("p (i d) -> p i d", i=2),
                              bias[:, 0:2 * D].rearrange("p (i d) -> p i d", i=2), ALU.add)
            dve.tensor_tensor(v_nat[:, t, :], ps[:, SIDE_BANK, 2 * D:3 * D], bias[:, 2 * D:3 * D],
                              ALU.add).then_inc(qkv_read, 1)

        def rest_of(dve, n, i):
            src = (qk, rest[0])[i][:].rearrange("p q t d -> p (q t d)")
            dve.wait_ge((p1_ready, p2_ready)[i], n.u + 1)
            if i == 1:
                dve.wait_ge(r1_ready, n.u + 1)
            dve.tensor_tensor(rest[i][:].rearrange("p q t d -> p (q t d)"), src,
                              part[i][:].rearrange("p q n d -> p (q n d)"), ALU.subtract
                              ).then_inc((r1_ready, r2_ready)[i], 1)

        def read_max(dve, w, s, i):
            dve.wait_ge(max_ps, MAXES * (STEPS * w.u + s) + i + 1)
            dve.tensor_reduce(mx[:, s % 2].rearrange("p t g -> p (t g)")[:, i:i + 1],
                              ps[:, MX_BANK + i % 2, :], AX_X, ALU.max).then_inc(max_read, 1)

        def split_max(dve, w, s):
            m, r, p = mx[:, s % 2], mr[:, s % 2], mp[:, s % 2]
            base = 4 * (STEPS * w.u + s)
            dve.wait_ge(max_read, MAXES * (STEPS * w.u + s + 1))
            if s >= 2:
                dve.wait_ge(mT_ps, STEPS * w.u + s - 1)
            dve.tensor_scalar(p[:, :, 0, :], m, -1.0, None, ALU.mult).then_inc(m_chain, 1)
            dve.wait_ge(m_chain, base + 1)
            dve.scalar_tensor_tensor(out=r, in0=m, scalar=-1.0, in1=p[:, :, 0, :], op0=ALU.mult,
                                     op1=ALU.subtract).then_inc(m_chain, 1)
            dve.wait_ge(m_chain, base + 2)
            dve.tensor_copy(p[:, :, 1, :], r).then_inc(m_chain, 1)
            dve.wait_ge(m_chain, base + 3)
            dve.tensor_tensor(r, r, p[:, :, 1, :], ALU.subtract).then_inc(m_chain, 1)
            dve.wait_ge(m_chain, base + 4)
            dve.tensor_copy(p[:, :, 2, :], r).then_inc(m_split, 1)

        def attention_out(dve, w):
            dve.wait_ge(oT_ps, w.u + 1)
            oT = ps[:, 4:6, :].rearrange("p k (n f) -> p (k n) f", f=P)
            dve.reciprocal(rden[:], oT.rearrange("p n (g f) -> p n g f", g=G)[:, :, :, 16:18]).then_inc(rden_ready, 1)
            dve.wait_ge(rden_ready, w.u + 1)
            for a in range(2):
                for c in range(2):
                    o = 16 * a + HD * c
                    src = oT.rearrange("p (t a) (g f) -> p a t g f", a=2, g=G)[:, a, :, :, HD * c:HD * c + HD]
                    dst = o_nat[:].rearrange("p t (g f) -> p t g f", g=G)[:, :, :, o:o + HD]
                    den = rden[:].rearrange("p (t a) g c -> p a c t g", a=2)[:, a, c]
                    last = dve.tensor_tensor(dst, src, den.unsqueeze(3).to_broadcast([P, NT, G, HD]), ALU.mult)
            last.then_inc(on_ready, 1)

        def gated(dve, w, i):
            L, NG = w.L, gate_ups(w.L)
            dve.wait_ge(up_ps[L], NG * w.b + i + 1)
            dve.wait_ge(silu_done[L], NG * w.b + i + 1)
            if L == 1 and i >= 2 * EB and i % EB == 0:
                dve.wait_ge(y_ps[1], (E + 1) * w.b + i // EB)
            dst = hT[:, 0, i, :] if L == 0 else hT[:, (i // EB) % 2, i % EB, :]
            dve.tensor_tensor(dst, ps[:, gu_bank(2 * i + 1), :], sil[:, i % 2, :], ALU.mult).then_inc(h_ready[L], 1)

        ROUTE_LINKS = 34

        def chain(dve, sem_, base):
            links = [0]

            def link(ins):
                links[0] += 1
                ins.then_inc(sem_, 1)
                dve.wait_ge(sem_, base + links[0])
            return link, links

        def wide(v):
            return v.unsqueeze(2).to_broadcast([P, NT, E])

        def choose_experts(dve, w, link):
            dve.wait_ge(logit_ps, w.b + 1)
            lg = ps[:, ROUTER_BANK, 0:NT * E].rearrange("p (t e) -> p t e", e=E)
            link(dve.tensor_reduce(r_s[:, 0], lg, AX_X, ALU.max))
            dve.tensor_tensor(r_t[:, 0], lg, wide(r_s[:, 0]), ALU.subtract).then_inc(lg_ready, 1)
            dve.wait_ge(rexp_done, w.b + 1)
            link(dve.tensor_reduce(r_s[:, 0], r_t[:, 1], AX_X, ALU.add))
            link(dve.reciprocal(r_s[:, 1], r_s[:, 0]))
            link(dve.tensor_tensor(r_p[:], r_t[:, 1], wide(r_s[:, 1]), ALU.mult))
            for k in range(2):
                link(dve.tensor_reduce(r_s[:, 2 + k], r_p[:], AX_X, ALU.max))
                link(dve.tensor_tensor(r_t[:, 2], r_p[:], wide(r_s[:, 2 + k]), ALU.is_equal))
                link(dve.scalar_tensor_tensor(out=r_t[:, 3], in0=r_t[:, 2], scalar=-99.0, in1=iota_hi[:],
                                              op0=ALU.mult, op1=ALU.add))
                link(dve.tensor_reduce(r_s[:, 4], r_t[:, 3], AX_X, ALU.min))
                link(dve.tensor_tensor(oh[:, :, k, :], iota_e[:], wide(r_s[:, 4]), ALU.is_equal))
                if k == 0:
                    link(dve.scalar_tensor_tensor(out=r_p[:], in0=oh[:, :, 0, :], scalar=-2.0, in1=r_p[:],
                                                  op0=ALU.mult, op1=ALU.add))
            dve.tensor_tensor(r_s[:, 0], r_s[:, 2], r_s[:, 3], ALU.add).then_inc(oh_ready, 1)
            dve.wait_ge(oh_ready, w.b + 1)
            link(dve.tensor_scalar(r_s[:, 1], r_s[:, 0], 1e-9, None, ALU.add))
            link(dve.reciprocal(r_s[:, 0], r_s[:, 1]))
            link(dve.tensor_tensor(r_s[:, 5:7], r_s[:, 2:4], r_s[:, 0:1].to_broadcast([P, 2, NT]), ALU.mult))

        def combine_weights(dve, w, link):
            dve.wait_ge(rank_ps, w.b + 1)
            NK = 2 * E
            link(dve.tensor_copy(tot[:].rearrange("p t k -> p (t k)"), ps[:, ROUTER_BANK, 128:128 + NT * NK]))
            for t in range(NT):
                link(dve.tensor_tensor(rk[:, t, :], ps[:, ROUTER_BANK, 64 + t * NK:64 + (t + 1) * NK],
                                       carry[:, t % 2, :], ALU.add))
                link(dve.tensor_tensor(carry[:, (t + 1) % 2, :], carry[:, t % 2, :], tot[:, t, :], ALU.add))
            rk4 = rk[:].rearrange("p t (k e) -> p t k e", e=E)
            for k in range(2):
                link(dve.tensor_scalar(r_t[:, 2], rk4[:, :, k, :], float(CAP), None, ALU.is_le))
                link(dve.tensor_tensor(r_t[:, 3], r_t[:, 2], oh[:, :, k, :], ALU.mult))
                dst = comb[:] if k == 0 else r_t[:, 0]
                link(dve.tensor_tensor(dst, r_t[:, 3], wide(r_s[:, 5 + k]), ALU.mult))
            link(dve.tensor_tensor(comb[:], comb[:], r_t[:, 0], ALU.add))

        def residual(dve, w, bank):
            dve.wait_ge(stored, 16 * w.u + 16)
            dve.wait_ge(x_taken, 2 * w.u + 2)
            return dve.tensor_tensor(x_out[:], ps[:, bank, :].rearrange("p (t d) -> p t d", d=D), x_in[:], ALU.add)

        def add_bias(dve, w):
            dve.tensor_tensor(x_out[:], x_out[:], b_proj[w.L][:].unsqueeze(1).to_broadcast([P, NT, D]),
                              ALU.add).then_inc(unit_done, 1)

        def vector_unit(dve, w, n):
            for s in range(STEPS):
                for k in range(NT):
                    for g in range(G):
                        read_max(dve, w, s, G * k + g)
                    if n is not None and (s, k) in ((3, 0), (3, 2), (3, 3)):
                        read_qkv(dve, n, {0: 0, 2: 1, 3: 2}[k])
                split_max(dve, w, s)
                if s == 1 and n is not None:
                    normalize(dve, n)
            if n is not None:
                read_qkv(dve, n, 3)
                for i in range(2):
                    rest_of(dve, n, i)

            def operands(j):
                if n is not None:
                    operand_copies(dve.tensor_copy, dve.wait_ge, n, 1, j)

            if w.L == 0:
                gated(dve, w, 0)
                attention_out(dve, w)
                for i in range(1, HB):
                    operands(i - 1)
                    gated(dve, w, i)
                operands(HB - 1)
                dve.wait_ge(y_ps[0], w.b + 1)
                residual(dve, w, 5).then_inc(out_chain[0], 1)
                dve.wait_ge(out_chain[0], w.b + 1)
                add_bias(dve, w)
                operands(HB)
            else:
                link, links = chain(dve, route_chain, ROUTE_LINKS * w.b)
                choose_experts(dve, w, link)
                gated(dve, w, 0)
                attention_out(dve, w)
                gated(dve, w, 1)
                combine_weights(dve, w, link)
                assert links[0] == ROUTE_LINKS, links[0]
                dve.wait_ge(y_ps[1], (E + 1) * w.b + 1)
                residual(dve, w, 5).then_inc(y_read, 1)
                for e in range(E):
                    if e + 1 < E:
                        for i in range(EB):
                            gated(dve, w, (e + 1) * EB + i)
                    if e < 4:
                        operands(e)
                    dve.wait_ge(y_ps[1], (E + 1) * w.b + e + 2)
                    dve.wait_ge(y_read, (E + 1) * w.b + e + 1)
                    for t in range(NT):
                        last = dve.scalar_tensor_tensor(
                            out=x_out[:, t, :], in0=ps[:, 4 + e % 2, t * P:(t + 1) * P],
                            scalar=comb[:, t, e:e + 1], in1=x_out[:, t, :], op0=ALU.mult, op1=ALU.add)
                    last.then_inc(y_read, 1)
                dve.wait_ge(y_read, (E + 1) * w.b + E + 1)
                add_bias(dve, w)

        def all_units(eng, unit):
            with eng.Fori(0, B - 1) as b:
                unit(eng, Unit(0, b), Unit(0, b + 1))
            unit(eng, Unit(0, B - 1), Unit(1, 0))
            with eng.Fori(0, B - 1) as b:
                unit(eng, Unit(1, b), Unit(1, b + 1))
            unit(eng, Unit(1, B - 1), None)

        FIRST = Unit(0, 0)
        block = ctx.enter_context(nc.Block())

        @block.sync
        def _(sp):
            load_x(sp, FIRST)
            first_setup_sync(sp)
            setup_sync(sp)
            sp.sem_inc(unit_done, 1)
            sp.sem_inc(stored, 16)
            sp.wait_ge(mask_ready, 1)
            sp.wait_ge(ready, 1)
            for h in range(H):
                sp.dma_start(KO[MASK_ROW:MASK_ROW + NB, h, :], onehot_k[:]).then_inc(key_rows_in, 16)
            with sp.Fori(0, B - 1) as b:
                sync_unit(sp, Unit(0, b), Unit(0, b + 1))
            sync_unit(sp, Unit(0, B - 1), Unit(1, 0))
            for h in range(H):
                sp.dma_start(QO[MASK_ROW:MASK_ROW + NB, h, :], mask_q[:]).then_inc(rows_in, 16)
            with sp.Fori(0, B - 1) as b:
                sync_unit(sp, Unit(1, b), Unit(1, b + 1))
            sync_unit(sp, Unit(1, B - 1), None)
            sp.wait_ge(stored, 16 * 2 * B + 16)

        @block.gpsimd
        def _(pool):
            setup_pool(pool)
            reciprocal_deviation(pool, FIRST)
            fill_slots(pool, FIRST)
            place_values_0(pool, FIRST)
            all_units(pool, pool_unit)

        @block.vector
        def _(dve):
            first_setup_vector(dve)
            normalize(dve, FIRST)
            for t in range(NT):
                read_qkv(dve, FIRST, t)
            for i in range(2):
                rest_of(dve, FIRST, i)
            for j in range(4):
                operand_copies(dve.tensor_copy, dve.wait_ge, FIRST, 1, j)
            setup_vector(dve)
            all_units(dve, vector_unit)

        @block.scalar
        def _(act):
            xnT_copy(act, FIRST)
            for i in range(3):
                cast_part(act, FIRST, i)
            for j in range(4):
                operand_copies(act.copy, act.wait_ge, FIRST, 0, j)
            all_units(act, scalar_unit)

        @block.tensor
        def _(pe):
            pe.wait_ge(consts, N_CONST)
            pe.wait_ge(cleared, N_CLEARED)
            pe.wait_ge(first_ready, 1)
            xnT_mms(pe, FIRST)
            for t in range(NT):
                qkv_mm(pe, FIRST, t)
            for j in range(4):
                for side in range(2):
                    operand_transposes(pe, FIRST, side, j)
            pe.wait_ge(ready, 1)
            pe.wait_ge(key_rows_in, 16 * H)
            with pe.Fori(0, B - 1) as b:
                tensor_unit(pe, Unit(0, b), Unit(0, b + 1))
            tensor_unit(pe, Unit(0, B - 1), Unit(1, 0))
            pe.wait_ge(rows_in, 16 * H)
            with pe.Fori(0, B - 1) as b:
                tensor_unit(pe, Unit(1, b), Unit(1, b + 1))
            tensor_unit(pe, Unit(1, B - 1), None)


def kernel(L0_attn_x, L0_attn_qkv_w, L0_attn_qkv_b, L0_attn_proj_w, L0_attn_proj_b, L0_ffn_w_gate, L0_ffn_w_up,
           L0_ffn_w_down, L1_attn_Wq, L1_attn_bq, L1_attn_Wk, L1_attn_bk, L1_attn_Wv, L1_attn_bv, L1_attn_Wo,
           L1_attn_bo, L1_attn_src_blocks, L1_attn_tgt_blocks, L1_ffn_gate_w, L1_ffn_gate_proj_w,
           L1_ffn_up_proj_w, L1_ffn_down_proj_w):
    import numpy as np
    import concourse.bacc as bacc
    from concourse.bass_utils import run_bass_kernel_spmd

    def T(a, *axes):
        return np.ascontiguousarray(np.transpose(np.asarray(a), axes or None))

    arrays = {
        "x": np.asarray(L0_attn_x),
        "qkv_wT": T(L0_attn_qkv_w), "qkv_b": np.asarray(L0_attn_qkv_b),
        "proj_wT": T(L0_attn_proj_w), "proj_b": np.asarray(L0_attn_proj_b),
        "wg_T": T(L0_ffn_w_gate), "wu_T": T(L0_ffn_w_up), "wd_T": T(L0_ffn_w_down),
        "Wq_T": T(L1_attn_Wq), "bq": np.asarray(L1_attn_bq),
        "Wk_T": T(L1_attn_Wk), "bk": np.asarray(L1_attn_bk),
        "Wv_T": T(L1_attn_Wv), "bv": np.asarray(L1_attn_bv),
        "Wo_T": T(L1_attn_Wo), "bo": np.asarray(L1_attn_bo),
        "src_blocks": np.asarray(L1_attn_src_blocks), "tgt_blocks": np.asarray(L1_attn_tgt_blocks),
        "router_T": T(L1_ffn_gate_w),
        "eg_T": T(L1_ffn_gate_proj_w, 2, 0, 1), "eu_T": T(L1_ffn_up_proj_w, 2, 0, 1),
        "ed_T": T(L1_ffn_down_proj_w, 0, 2, 1),
    }
    nc = bacc.Bacc("TRN2", target_bir_lowering=False, num_devices=1)
    args = {n: nc.dram_tensor("in_" + n, a.shape, mybir.dt.from_np(a.dtype), kind="ExternalInput").ap()
            for n, a in arrays.items()}
    out = nc.dram_tensor("out_y", arrays["x"].shape, F32, kind="ExternalOutput").ap()
    build(nc, out=out, **args)
    r = run_bass_kernel_spmd(nc, [{"in_" + n: a for n, a in arrays.items()}], core_ids=[0])
    return r.results[0]["out_y"]
```

```python
from contextlib import ExitStack

import concourse.bass as bass
from concourse import mybir

F32 = mybir.dt.float32
BF16 = mybir.dt.bfloat16
I32 = mybir.dt.int32
ALU = mybir.AluOpType
ACT = mybir.ActivationFunctionType
AX_X = mybir.AxisListType.X

P = 128
EPS = 1e-5
MASKED = -1e30


def build(nc, x, qkv_wT, qkv_b, proj_wT, proj_b, wg_T, wu_T, wd_T, Wq_T, bq, Wk_T, bk, Wv_T, bv, Wo_T, bo,
          src_blocks, tgt_blocks, router_T, eg_T, eu_T, ed_T, out):
    B, S, D = x.shape
    H, HD = 16, 8
    NT = S // P
    G = 4
    STEPS = H // G
    HID = wg_T.shape[1]
    HB = HID // P
    E, EH = eg_T.shape[1], eg_T.shape[2]
    EB = EH // P
    T = B * S
    CAP = int(1.25 * T / E)
    NB = S // 64
    SLOT = 64
    ROWS = 96
    M_ROW, MASK_ROW = 48, 64
    QSCALE = HD ** -0.5
    NSRC = src_blocks.shape[0]

    x_mid = nc.dram_tensor("x_mid", (B, S, D), F32, kind="Internal").ap()
    v_bounce = nc.dram_tensor("v_bounce", (S, D), F32, kind="Internal").ap()

    with ExitStack() as ctx:
        def sb(name, shape, dt=F32):
            return ctx.enter_context(nc.sbuf_tensor(name, shape, dt))

        def sem(name):
            return ctx.enter_context(nc.semaphore(name))

        ident = sb("ident", [P, P])
        ident_bf = sb("ident_bf", [P, P], BF16)
        zero_b = sb("zero_b", [P, 1], BF16)
        tri = sb("tri", [P, P], BF16)
        ones_bf = sb("ones_bf", [P, P], BF16)
        w_qkv = [sb("w_qkv0", [P, 3 * D]), sb("w_qkv1", [P, 3 * D])]
        b_qkv = [sb("b_qkv0", [P, 3 * D]), sb("b_qkv1", [P, 3 * D])]
        w_proj = [sb("w_proj0", [P, D]), sb("w_proj1", [P, D])]
        b_proj = [sb("b_proj0", [P, D]), sb("b_proj1", [P, D])]
        wg_i = sb("wg_i", [P, HID], I32)
        wu_i = sb("wu_i", [P, HID], I32)
        wd_i = sb("wd_i", [P, HB, D], I32)
        wg = sb("wg", [P, HID])
        wu = sb("wu", [P, HID])
        wd = sb("wd", [P, HB, D])
        w_router = sb("w_router", [P, E])
        eg = sb("eg", [P, E, EH])
        eu = sb("eu", [P, E, EH])
        ed = sb("ed", [P, E, EB, D])
        st_i = sb("st_i", [NB, 2, NSRC], I32)
        st_f = sb("st_f", [NB, 2, NSRC])
        blk_q = sb("blk_q", [NB, NB])
        blk_k = sb("blk_k", [NB, NB])
        hits = sb("hits", [NB, NB])
        tmp8 = sb("tmp8", [NB, 4, NB])
        mask_q = sb("mask_q", [NB, S], BF16)
        onehot_k = sb("onehot_k", [NB, S], BF16)
        x_next = sb("x_next", [P, NT, D])
        xnT_next = sb("xnT_next", [P, S])
        x_in = sb("x_in", [P, NT, D])
        x_out = sb("x_out", [P, NT, D])
        stats = sb("stats", [P, NT, 6])
        mv = sb("mv", [P, NT, 2])
        rstd = sb("rstd", [P, NT])
        var_eps = sb("var_eps", [P, NT])
        eps_t = sb("eps_t", [P, NT])
        neg_half = sb("neg_half", [P, NT])
        wait_taker = sb("wait_taker", [P, NT])
        pool_taker = sb("pool_taker", [P, 5, NT])
        xn = sb("xn", [P, NT, D])
        xnT = sb("xnT", [P, S])
        qk = sb("qk", [P, 2, NT, D])
        part = [sb(f"part{i}", [P, 2, NT * H, HD], BF16) for i in range(3)]
        rest = [sb(f"rest{i}", [P, 2, NT, D]) for i in range(2)]
        v_nat = sb("v_nat", [P, NT, D])
        Rq = sb("Rq", [P, NT * H, SLOT], BF16)
        Rk = sb("Rk", [P, NT * H, SLOT], BF16)
        QO = sb("QO", [ROWS, H, S], BF16)
        KO = sb("KO", [ROWS, H, S], BF16)
        Vp = sb("Vp", [P, NT, H, 32])
        PT = sb("PT", [P, 4, 2, S])
        mx = sb("mx", [P, 2, NT, G])
        mr = sb("mr", [P, 2, NT, G])
        mp = sb("mp", [P, 2, NT, 3, G], BF16)
        mT = sb("mT", [3 * G, 2, S], BF16)
        o_sb = sb("o_sb", [P, 2, S])
        rden = sb("rden", [P, NT * 2, G, 2])
        o_nat = sb("o_nat", [P, NT, D])
        o_T = sb("o_T", [P, S])
        sil = sb("sil", [P, 2, S])
        hT = sb("hT", [P, 2, max(HB, EB), S])
        iota_e = sb("iota_e", [P, NT, E])
        iota_hi = sb("iota_hi", [P, NT, E])
        r_p = sb("r_p", [P, NT, E])
        r_t = sb("r_t", [P, 4, NT, E])
        r_s = sb("r_s", [P, 8, NT])
        oh = sb("oh", [P, NT, 2, E], BF16)
        rk = sb("rk", [P, NT, 2 * E])
        tot = sb("tot", [P, NT, 2 * E])
        carry = sb("carry", [P, 2, 2 * E])
        comb = sb("comb", [P, NT, E])

        ps = ctx.enter_context(nc.psum_tensor("ps", [P, 8, 512], F32))

        def ps_bf(bank):
            return ps[:, bank, :].bitcast(BF16)

        MX_BANK, PV_BANK, SIDE_BANK = 4, 6, 7
        ROUTER_BANK, FIRST_MX_BANK = 3, 6
        K_BANK = 0
        LOGIT_BANK = 5

        loaded = sem("loaded")
        first_loaded = sem("first_loaded")
        first_ready = sem("first_ready")
        operands_cleared = sem("operands_cleared")
        zeros = sem("zeros")
        consts = sem("consts")
        cleared = sem("cleared")
        dve_setup = sem("dve_setup")
        ready = sem("ready")
        pool_setup = sem("pool_setup")
        rows_in = sem("rows_in")
        key_rows_in = sem("key_rows_in")
        mask_ready = sem("mask_ready")

        first_loads = [(w_qkv[0][:], qkv_wT), (b_qkv[0][:], qkv_b[None, :].to_broadcast([P, 3 * D]))]
        loads = [(w_proj[0][:], proj_wT), (b_proj[0][:], proj_b[None, :].to_broadcast([P, D])),
                 (wg_i[:], wg_T), (wu_i[:], wu_T), (wd_i[:], wd_T.rearrange("(b p) d -> p b d", p=P)),
                 (w_proj[1][:], Wo_T), (b_proj[1][:], bo[None, :].to_broadcast([P, D])),
                 (w_router[:], router_T), (eg[:], eg_T), (eu[:], eu_T),
                 (ed[:], ed_T.rearrange("e (b p) d -> p e b d", p=P)),
                 (st_i[:, 0, :], src_blocks[None, :].to_broadcast([NB, NSRC])),
                 (st_i[:, 1, :], tgt_blocks[None, :].to_broadcast([NB, NSRC]))]
        for i, (w, b) in enumerate(((Wq_T, bq), (Wk_T, bk), (Wv_T, bv))):
            loads.append((w_qkv[1][:, i * D:(i + 1) * D], w))
            loads.append((b_qkv[1][:, i * D:(i + 1) * D], b[None, :].to_broadcast([P, D])))
        N_LOAD = 16 * len(loads)
        N_FIRST = 16 * len(first_loads)

        def first_setup_sync(sp):
            for dst, src in first_loads:
                sp.dma_start(dst, src).then_inc(first_loaded, 16)

        def setup_sync(sp):
            for dst, src in loads:
                sp.dma_start(dst, src).then_inc(loaded, 16)

        def first_setup_pool(pool):
            pool.memset(zero_b[:], 0.0).then_inc(zeros, 1)
            pool.memset(eps_t[:], EPS).then_inc(zeros, 1)
            pool.memset(neg_half[:], -0.5).then_inc(zeros, 1)
            pool.wait_ge(zeros, N_ZERO)
            for n, t in enumerate((ident, ident_bf)):
                pool.memset(t[:], 0.0).then_inc(consts, 1)
                pool.wait_ge(consts, 2 * n + 1)
                pool.affine_select(out=t[:], in_=t[:], compare_op=ALU.not_equal, fill=1.0, base=0,
                                   pattern=[[-1, P]], channel_multiplier=1).then_inc(consts, 1)

        def setup_pool(pool):
            pool.memset(tri[:], 1.0).then_inc(consts, 1)
            pool.wait_ge(consts, 5)
            pool.affine_select(out=tri[:], in_=tri[:], compare_op=ALU.is_ge, fill=0.0, base=0,
                               pattern=[[1, P]], channel_multiplier=-1).then_inc(consts, 1)
            pool.memset(ones_bf[:], 1.0).then_inc(consts, 1)
            pool.iota(iota_e[:], pattern=[[0, NT], [1, E]], base=0, channel_multiplier=0,
                      allow_small_or_imprecise_dtypes=True).then_inc(consts, 1)
            pool.iota(iota_hi[:], pattern=[[0, NT], [1, E]], base=99, channel_multiplier=0,
                      allow_small_or_imprecise_dtypes=True).then_inc(consts, 1)
            pool.iota(blk_q[:], pattern=[[1, NB]], base=0, channel_multiplier=0,
                      allow_small_or_imprecise_dtypes=True).then_inc(consts, 1)
            pool.iota(blk_k[:], pattern=[[0, NB]], base=0, channel_multiplier=1,
                      allow_small_or_imprecise_dtypes=True).then_inc(consts, 1)
            pool.memset(onehot_k[:], 1.0).then_inc(consts, 1)
            pool.wait_ge(consts, 12)
            pool.affine_select(out=onehot_k[:], in_=onehot_k[:], compare_op=ALU.is_ge, fill=0.0, base=0,
                               pattern=[[1, S]], channel_multiplier=-64).then_inc(consts, 1)
            pool.wait_ge(consts, 13)
            pool.affine_select(out=onehot_k[:], in_=onehot_k[:], compare_op=ALU.is_ge, fill=0.0, base=63,
                               pattern=[[-1, S]], channel_multiplier=64).then_inc(consts, 1)
            pool.memset(Rk[:], 0.0).then_inc(cleared, 1)
            pool.memset(Rq[:], 0.0).then_inc(cleared, 1)
            pool.wait_ge(cleared, 2)
            pool.memset(Rk[:, :, M_ROW:M_ROW + 3], 1.0).then_inc(cleared, 1)
            pool.memset(Vp[:], 0.0).then_inc(cleared, 1)
            pool.wait_ge(cleared, 4)
            for c in range(2):
                pool.memset(Vp[:].rearrange("p t (a c g) f -> p c (t a) g f", c=2, g=G)[:, c, :, :, 16 + c:17 + c],
                            1.0).then_inc(cleared, 1)
            pool.wait_ge(cleared, N_CLEARED)

        N_ZERO, N_IDENT, N_CONST, N_CLEARED = 3, 4, 14, 6

        def scale_q(eng, layer):
            eng.tensor_scalar(w_qkv[layer][:, 0:D], w_qkv[layer][:, 0:D], QSCALE, None, ALU.mult)
            return eng.tensor_scalar(b_qkv[layer][:, 0:D], b_qkv[layer][:, 0:D], QSCALE, None, ALU.mult)

        def first_setup_vector(dve):
            dve.wait_ge(first_loaded, N_FIRST)
            scale_q(dve, 0).then_inc(first_ready, 1)
            dve.wait_ge(first_ready, 1)
            dve.memset(KO[64:96], 0.0).then_inc(operands_cleared, 1)

        def setup_scalar(act):
            act.wait_ge(zeros, N_ZERO)
            act.copy(QO[64:96], zero_b[64:96].unsqueeze(2).to_broadcast([32, H, S])).then_inc(operands_cleared, 1)

        def setup_vector(dve):
            n = [0]

            def link(ins):
                n[0] += 1
                ins.then_inc(dve_setup, 1)
                dve.wait_ge(dve_setup, n[0])

            dve.memset(carry[:], 0.0).then_inc(dve_setup, 1)
            n[0] += 1
            dve.wait_ge(loaded, N_LOAD)
            link(dve.tensor_copy(st_f[:], st_i[:]))
            dve.wait_ge(consts, N_CONST)
            link(dve.tensor_tensor(tmp8[:, 0, :], blk_q[:], blk_k[:], ALU.subtract))
            link(dve.tensor_tensor(tmp8[:, 1, :], tmp8[:, 0, :], tmp8[:, 0, :], ALU.mult))
            link(dve.tensor_scalar(hits[:], tmp8[:, 1, :], 1.0, None, ALU.is_le))
            for j in (0, NB - 1):
                link(dve.tensor_scalar(tmp8[:, 0, :], blk_k[:], float(j), None, ALU.is_equal))
                link(dve.tensor_tensor(hits[:], hits[:], tmp8[:, 0, :], ALU.add))
            for n_pair in range(NSRC):
                for side, blk in ((0, blk_q), (1, blk_k)):
                    v = st_f[:, side, n_pair:n_pair + 1]
                    link(dve.tensor_scalar(tmp8[:, 2, :], blk[:], v, None, ALU.is_equal))
                    link(dve.tensor_scalar(tmp8[:, 3, :], blk[:], float(NB), v, ALU.subtract, ALU.is_equal))
                    link(dve.tensor_tensor(tmp8[:, side, :], tmp8[:, 2, :], tmp8[:, 3, :], ALU.add))
                link(dve.tensor_tensor(tmp8[:, 0, :], tmp8[:, 0, :], tmp8[:, 1, :], ALU.mult))
                link(dve.tensor_tensor(hits[:], hits[:], tmp8[:, 0, :], ALU.add))
            link(dve.tensor_scalar(hits[:], hits[:], 0.5, MASKED, ALU.is_lt, ALU.mult))
            dve.tensor_copy(mask_q[:].rearrange("p (b t) -> p b t", b=NB),
                            hits[:].unsqueeze(2).to_broadcast([NB, NB, 64])).then_inc(mask_ready, 1)

        def dequantize(pool):
            pool.wait_ge(loaded, N_LOAD)
            for n_w, (i, f) in enumerate(((wg_i, wg), (wu_i, wu), (wd_i, wd))):
                pool.tensor_copy(f[:], i[:]).then_inc(pool_setup, 1)
                pool.wait_ge(pool_setup, n_w + 1)
                pool.tensor_scalar(f[:], f[:], 1.0 / 127.0, None, ALU.mult)
            scale_q(pool, 1).then_inc(ready, 1)

        x_loaded = sem("x_loaded")
        x_taken = sem("x_taken")
        stats_done = sem("stats_done")
        mv_ready = sem("mv_ready")
        rstd_ready = sem("rstd_ready")
        xn_ready = sem("xn_ready")
        xnT_ps = sem("xnT_ps")
        xnT_ready = sem("xnT_ready")
        qkv_ps = sem("qkv_ps")
        qkv_read = sem("qkv_read")
        v_stored = sem("v_stored")
        v_loaded = sem("v_loaded")
        v_placed = sem("v_placed")
        p1_ready = sem("p1_ready")
        p2_ready = sem("p2_ready")
        p3_ready = sem("p3_ready")
        r1_ready = sem("r1_ready")
        r2_ready = sem("r2_ready")
        R1_ready = sem("R1_ready")
        R_ready = sem("R_ready")
        q_ps = sem("q_ps")
        k_ps = sem("k_ps")
        q_copied = sem("q_copied")
        k_copied = sem("k_copied")
        max_ps = sem("max_ps")
        max_read = sem("max_read")
        m_chain = sem("m_chain")
        m_split = sem("m_split")
        mT_ps = sem("mT_ps")
        mT_ready = sem("mT_ready")
        m_rows = sem("m_rows")
        st_ps = sem("st_ps")
        exp_done = sem("exp_done")
        pv_done = sem("pv_done")
        o_copied = sem("o_copied")
        oT_ps = sem("oT_ps")
        rden_ready = sem("rden_ready")
        on_ready = sem("on_ready")
        onT_ps = sem("onT_ps")
        onT_ready = sem("onT_ready")
        unit_done = sem("unit_done")
        stored = sem("stored")
        gate_ps = [sem(f"gate_ps{i}") for i in range(2)]
        up_ps = [sem(f"up_ps{i}") for i in range(2)]
        silu_done = [sem(f"silu_done{i}") for i in range(2)]
        h_ready = [sem(f"h_ready{i}") for i in range(2)]
        y_ps = [sem(f"y_ps{i}") for i in range(2)]
        logit_ps = sem("logit_ps")
        lg_ready = sem("lg_ready")
        rexp_done = sem("rexp_done")
        oh_ready = sem("oh_ready")
        rank_ps = sem("rank_ps")
        route_chain = sem("route_chain")
        y_read = sem("y_read")

        EXPS = 2 * NT
        M_DMAS = 3
        V_DMAS = 16 * NT * STEPS
        MAXES = NT * G

        def head(s, g):
            return G * s + g

        def max_bank(s, i):
            return (FIRST_MX_BANK if s < 2 else MX_BANK) + i % 2

        def qkv_bank(n, t):
            return t if n is FIRST else SIDE_BANK

        def operand_bank(n, side, j):
            if j < 2:
                return MX_BANK + side
            return K_BANK if side == 1 and n.beside == 0 else ROUTER_BANK

        def turned_max_bank(s):
            return ROUTER_BANK if s == 0 else SIDE_BANK

        def gate_ups(L):
            return HB if L == 0 else E * EB

        def gate_up_weights(L, n):
            if L == 0:
                return wg[:, n * P:(n + 1) * P], wu[:, n * P:(n + 1) * P]
            e, i = n // EB, n % EB
            return eg[:, e, i * P:(i + 1) * P], eu[:, e, i * P:(i + 1) * P]

        def gu_bank(m):
            return m % 3

        class Unit:

            def __init__(self, L, b, beside=None):
                self.L, self.b, self.u = L, b, B * L + b
                self.beside = L if beside is None else beside

        FIRST = Unit(0, 0)

        def load_x(sp, n):
            if n.L == 1:
                sp.wait_ge(stored, 16 * n.b + 32)
            src = (x if n.L == 0 else x_mid)[n.b]
            sp.dma_start(x_next[:], src.rearrange("(t p) d -> p t d", p=P)).then_inc(x_loaded, 16)

        def max_rows_in(sp, w, s):
            sp.wait_ge(mT_ready, STEPS * w.u + s + 1)
            for i in range(3):
                sp.dma_start(QO[M_ROW + i:M_ROW + i + 1, G * s:G * s + G, :],
                             mT[G * i:G * i + G, s % 2, :]).then_inc(m_rows, 16)

        def place_values_1(sp, n):
            sp.wait_ge(pv_done, NT * STEPS * n.u)
            sp.wait_ge(qkv_read, NT * n.u + NT)
            sp.dma_start(v_bounce.rearrange("(t p) d -> p t d", p=P), v_nat[:]).then_inc(v_stored, 16)
            sp.wait_ge(v_stored, 16 * n.b + 16)
            v_pos = v_bounce.rearrange("(h k t) (c d) -> k (t c) h d", h=H, k=NT, c=H)
            for k in range(NT):
                for s in range(STEPS):
                    heads, c = slice(G * s, G * s + G), s % 2
                    sp.dma_start(Vp[:, k, heads, HD * c:HD * c + HD], v_pos[k][:, heads, :]).then_inc(v_loaded, 16)

        def store_x(sp, w):
            sp.wait_ge(unit_done, w.u + 2)
            dst = (x_mid if w.L == 0 else out)[w.b]
            sp.dma_start(dst.rearrange("(t p) d -> p t d", p=P), x_out[:]).then_inc(stored, 16)

        def sync_unit(sp, w, n):
            if n is not None:
                sp.wait_ge(x_taken, 2 * w.u + 2)
                load_x(sp, n)
            for s in range(1, STEPS):
                max_rows_in(sp, w, s)
            if n is not None and n.L == 1:
                place_values_1(sp, n)
            if n is not None and w.L == 1:
                max_rows_in(sp, n, 0)
            store_x(sp, w)
            if n is not None and w.L == 0:
                max_rows_in(sp, n, 0)

        def reciprocal_deviation(pool, n):
            pool.wait_ge(mv_ready, n.u + 1)
            pool.tensor_tensor(var_eps[:], mv[:, :, 1], eps_t[:], ALU.add).then_inc(rstd_ready, 1)
            pool.wait_ge(rstd_ready, 2 * n.u + 1)
            pool.tensor_tensor(rstd[:], var_eps[:], neg_half[:], ALU.pow).then_inc(rstd_ready, 1)

        def take_x(pool, w):
            pool.wait_ge(unit_done, w.u + 1)
            pool.tensor_tensor(pool_taker[:, 0], eps_t[:], eps_t[:], ALU.add)
            pool.tensor_tensor(x_in[:], x_next[:], b_proj[w.L][:].unsqueeze(1).to_broadcast([P, NT, D]),
                               ALU.add).then_inc(x_taken, 1)
            pool.tensor_copy(xnT[:], xnT_next[:]).then_inc(x_taken, 1)

        def fill_slots(pool, n):
            pool.wait_ge(p3_ready, n.u + 1)
            pool.tensor_tensor(pool_taker[:, 1], eps_t[:], eps_t[:], ALU.add)
            slot_copy(pool, n, 2, 0).then_inc(R_ready, 1)

        def place_values_0(pool, n):
            if n is not FIRST:
                pool.wait_ge(pv_done, NT * STEPS * n.u)
                pool.tensor_tensor(pool_taker[:, 4], eps_t[:], eps_t[:], ALU.add)
            for c in range(2):
                src = v_nat[:].rearrange("p t (a c g d) -> p c (t a) g d", a=2, c=2, g=G)[:, c]
                dst = Vp[:].rearrange("p t (a c g) f -> p c (t a) g f", c=2, g=G)[:, c, :, :, HD * c:HD * c + HD]
                pool.tensor_copy(dst, src).then_inc(v_placed, 1)

        def pool_unit(pool, w, n):
            take_x(pool, w)
            if n is not None:
                reciprocal_deviation(pool, n)
                fill_slots(pool, n)
                if n.L == 0:
                    place_values_0(pool, n)

        def xnT_mms(pe, n):
            pe.wait_ge(xn_ready, n.u + 1)
            for t in range(NT):
                last = pe.transpose(ps[:, SIDE_BANK, t * P:(t + 1) * P], xn[:, t, :], ident[:])
            last.then_inc(xnT_ps, 1)

        def qkv_mm(pe, n, t):
            if t == 0:
                pe.wait_ge(xnT_ready, n.u + 1)
            elif n is not FIRST:
                pe.wait_ge(qkv_read, NT * n.u + t)
            pe.matmul(ps[:, qkv_bank(n, t), 0:3 * D], xnT_next[:, t * P:(t + 1) * P], w_qkv[n.L][:],
                      start=True, stop=True).then_inc(qkv_ps, 1)

        def operand_transposes(pe, n, side, j):
            ps_done, copied, other, R = ((q_ps, q_copied, k_copied, Rq), (k_ps, k_copied, q_copied, Rk))[side]
            bank = operand_bank(n, side, j)
            if (side, j) == (0, 0):
                pe.wait_ge(R1_ready, 5 * n.u + 5)
                pe.wait_ge(R_ready, n.u + 1)
            if j == 1 or (j == 3 and n.beside == 0):
                pe.wait_ge(copied, 8 * n.u + 2 * j)
            elif j >= 2 and (side, j) != (0, 2) and n.beside == 1:
                pe.wait_ge(other, 8 * n.u + (2 * j + 2 if side == 1 else 2 * j))
            Rv = R[:].rearrange("p (t h) s -> p t (h s)", t=NT)
            for i in range(2 * NT):
                t, c = (i % NT, G * j + 2 * (i // NT)) if n.L == 0 else (j, 2 * i)
                last = pe.transpose(ps_bf(bank)[:, i * P:(i + 1) * P], Rv[:, t, c * SLOT:(c + 2) * SLOT], ident_bf[:])
            last.then_inc(ps_done, 1)

        def max_mm(pe, w, s, i):
            qt, g = i // G, i % G
            if s == 0 and i == 0:
                if w.L == 1:
                    pe.wait_ge(rows_in, 16)
                pe.wait_ge(q_copied, 8 * w.u + 4)
                pe.wait_ge(k_copied, 8 * w.u + 4)
            if s == 2 and i == 0:
                pe.wait_ge(q_copied, 8 * w.u + 8)
                pe.wait_ge(k_copied, 8 * w.u + 8)
            if s > 0 or i >= 2:
                pe.wait_ge(max_read, MAXES * (STEPS * w.u + s) + i - 1)
            h = head(s, g)
            pe.matmul(ps[:, max_bank(s, i), :], QO[:, h, qt * P:(qt + 1) * P], KO[:, h, :],
                      start=True, stop=True).then_inc(max_ps, 1)

        def max_transposes(pe, w, s):
            pe.wait_ge(m_split, STEPS * w.u + s + 1)
            if s == 0:
                pe.wait_ge(k_copied, 8 * w.u + 8)
            for t in range(NT):
                last = pe.transpose(ps_bf(turned_max_bank(s))[0:3 * G, t * P:(t + 1) * P],
                                    mp[:, s % 2, t].rearrange("p i g -> p (i g)"), ident_bf[:])
            last.then_inc(mT_ps, 1)

        def score_mm(pe, w, s, k, g):
            i = 2 * k + g // 2
            if g % 2 == 0 and (s > 0 or i >= 2):
                pe.wait_ge(exp_done, EXPS * (STEPS * w.u + s) + i - 1)
            h = head(s, g)
            mm = pe.matmul(ps[:, 2 * (i % 2) + g % 2, :], KO[:, h, k * P:(k + 1) * P], QO[:, h, :],
                           start=True, stop=True)
            if g % 2 == 1:
                mm.then_inc(st_ps, 1)

        def value_mms(pe, w, s, k):
            pe.wait_ge(exp_done, EXPS * (STEPS * w.u + s) + 2 * k + 2)
            if s == 2 and k == 0:
                pe.wait_ge(o_copied, 2 * w.u + 1)
            if s == 0 and k == 0:
                if w.L == 0:
                    pe.wait_ge(v_placed, 2 * w.u + 2)
                else:
                    pe.wait_ge(v_loaded, V_DMAS * (w.b + 1))
            for g in range(G):
                last = pe.matmul(ps[32 * g:32 * g + 32, PV_BANK, :], Vp[:, k, head(s, g), :],
                                 PT[:, (2 * k + g // 2) % 4, g % 2, :],
                                 start=(s % 2 == 0 and k == 0), stop=(s % 2 == 1 and k == NT - 1))
            last.then_inc(pv_done, 1)

        def gate_up(pe, w, i, between=None):
            L, NG = w.L, gate_ups(w.L)
            for m, weight, done in ((2 * i, gate_up_weights(L, i)[0], gate_ps), (2 * i + 1, gate_up_weights(L, i)[1], up_ps)):
                before = m - 3
                if before >= 0:
                    pe.wait_ge((h_ready if before % 2 else silu_done)[L], NG * w.b + before // 2 + 1)
                pe.matmul(ps[:, gu_bank(m), :], weight, xnT[:], start=True, stop=True).then_inc(done[L], 1)
                if between is not None and m % 2 == 0:
                    between()

        def out_transposes(pe, w):
            for t in range(NT):
                for a in range(2):
                    c0 = ((t % 2) * 2 + a) * P
                    last = pe.transpose(ps[:, 4 + t // 2, c0:c0 + P], o_sb[:, a, t * P:(t + 1) * P], ident[:])
            last.then_inc(oT_ps, 1)

        def normalized_transposes(pe, w):
            pe.wait_ge(on_ready, w.u + 1)
            for t in range(NT):
                last = pe.transpose(ps[:, 4, t * P:(t + 1) * P], o_nat[:, t, :], ident[:])
            last.then_inc(onT_ps, 1)

        def out_mms_0(pe, w):
            pe.wait_ge(onT_ready, w.u + 1)
            pe.wait_ge(h_ready[0], HB * w.b + HB)
            for t in range(NT):
                tok = slice(t * P, (t + 1) * P)
                pe.matmul(ps[:, 5, tok], o_T[:, tok], w_proj[0][:], start=True, stop=False)
                for i in range(HB):
                    last = pe.matmul(ps[:, 5, tok], hT[:, 0, i, tok], wd[:, i, :], start=False, stop=(i == HB - 1))
                if t == NT - 1:
                    last.then_inc(y_ps[0], 1)
                yield t

        def out_mms_1(pe, w):
            pe.wait_ge(onT_ready, w.u + 1)
            for t in range(NT):
                tok = slice(t * P, (t + 1) * P)
                last = pe.matmul(ps[:, 5, tok], o_T[:, tok], w_proj[1][:], start=True, stop=True)
            last.then_inc(y_ps[1], 1)

        def router_mms(pe, w):
            pe.wait_ge(x_taken, 2 * w.u + 2)
            pe.wait_ge(max_read, MAXES * (STEPS * w.u + STEPS))
            for t in range(NT):
                last = pe.matmul(ps[:, LOGIT_BANK, t * E:(t + 1) * E], xnT[:, t * P:(t + 1) * P], w_router[:],
                                 start=True, stop=True)
            last.then_inc(logit_ps, 1)

        def rank_mms(pe, w):
            pe.wait_ge(oh_ready, w.b + 1)
            oh2 = oh[:].rearrange("p t k e -> p (t k e)")
            n_oh = NT * 2 * E
            pe.matmul(ps[:, ROUTER_BANK, 64:64 + n_oh], tri[:], oh2, start=True, stop=True)
            pe.matmul(ps[:, ROUTER_BANK, 128:128 + n_oh], ones_bf[:], oh2,
                      start=True, stop=True).then_inc(rank_ps, 1)

        def expert_out(pe, w, e):
            pe.wait_ge(h_ready[1], E * EB * w.b + (e + 1) * EB)
            if e >= 1:
                pe.wait_ge(y_read, E * w.b + e)
            for t in range(NT):
                tok = slice(t * P, (t + 1) * P)
                for i in range(EB):
                    last = pe.matmul(ps[:, 4 + e % 2, tok], hT[:, e % 2, i, tok], ed[:, e, i, :],
                                     start=(i == 0), stop=(i == EB - 1))
            last.then_inc(y_ps[1], 1)

        TURNS = ((0, 1), (1, 0), (2, 0))

        def side_mms(pe, w, n, s, k):
            if (w.L, s, k) == (1, 2, 0):
                router_mms(pe, w)
            if (s, k) in TURNS:
                if n is not None and s == 1:
                    pe.wait_ge(xnT_ready, n.u + 1)
                if n is not None and s == 2:
                    pe.wait_ge(qkv_read, NT * n.u + 3)
                max_transposes(pe, w, s + 1)
            if n is not None:
                if (s, k) == (0, 3):
                    pe.wait_ge(mT_ready, STEPS * w.u + 2)
                    xnT_mms(pe, n)
                tiles = {(1, 1): 0, (1, 2): 1, (1, 3): 2, (2, 1): 3}
                if (s, k) in tiles:
                    if k == 1:
                        pe.wait_ge(mT_ready, STEPS * w.u + s + 2)
                    qkv_mm(pe, n, tiles[s, k])
                if (s, k) in ((3, 2), (3, 3)):
                    if (w.L, k) == (1, 2):
                        pe.wait_ge(lg_ready, w.b + 1)
                    for side in range(2):
                        operand_transposes(pe, n, side, k - 2)

        def first_maxima(pe, n, i):
            if n is not None:
                max_mm(pe, n, i // MAXES, i % MAXES)
                if i == (MAXES + 6 if n.beside == 0 else 2 * MAXES - 4):
                    max_transposes(pe, n, 0)

        ROUTE_LINKS = 34

        def tensor_unit(pe, w, n):
            pe.wait_ge(mT_ready, STEPS * w.u + 1)
            for s in range(STEPS):
                pe.wait_ge(m_rows, 16 * M_DMAS * (STEPS * w.u + s + 1))
                for k in range(NT):
                    ahead = 0
                    if (s, k) == (0, 0):
                        ahead = G
                        for g in range(G):
                            score_mm(pe, w, s, k, g)
                        pe.wait_ge(max_read, MAXES * (STEPS * w.u + 2))
                        pe.wait_ge(unit_done, w.u + 1)
                    for g in range(G):
                        if s + 2 < STEPS:
                            max_mm(pe, w, s + 2, G * k + g)
                        if g >= ahead:
                            score_mm(pe, w, s, k, g)
                    side_mms(pe, w, n, s, k)
                    if k > 0:
                        value_mms(pe, w, s, k - 1)
                value_mms(pe, w, s, NT - 1)

            def operands(side, j):
                if n is not None:
                    operand_transposes(pe, n, side, j)

            def maxima(a, z):
                for i in range(a, z):
                    first_maxima(pe, n, i)

            pe.wait_ge(x_taken, 2 * w.u + 2)
            pe.wait_ge(ready, 1)
            gate_up(pe, w, 0)
            if w.L == 1:
                rank_mms(pe, w)
            gate_up(pe, w, 1)
            pe.wait_ge(o_copied, 2 * w.u + 2)
            maxima(0, 2)
            out_transposes(pe, w)
            if w.L == 0:
                maxima(2, 4)
                gate_up(pe, w, 2, lambda: maxima(4, 5))
                operands(0, 2)
                maxima(5, 7)
                pe.wait_ge(h_ready[0], HB * w.b + 2)
                operands(1, 2)
                maxima(7, 9)
                normalized_transposes(pe, w)
                maxima(9, 12)
                operands(0, 3)
                maxima(12, 14)
                operands(1, 3)
                maxima(14, 17)
                for t in out_mms_0(pe, w):
                    maxima(17 + 2 * t, 19 + 2 * t)
                maxima(25, 32)
            else:
                maxima(2, 4)
                gate_up(pe, w, 2)
                maxima(4, 6)
                normalized_transposes(pe, w)
                gate_up(pe, w, 3)
                maxima(6, 8)
                out_mms_1(pe, w)
                for e in range(E):
                    expert_out(pe, w, e)
                    if e + 2 < E:
                        at = 8 + 4 * e
                        gate_up(pe, w, (e + 2) * EB)
                        maxima(at, at + 2)
                        gate_up(pe, w, (e + 2) * EB + 1)
                        if e == 0:
                            pe.wait_ge(route_chain, ROUTE_LINKS * (w.b + 1))
                        if e < 4:
                            operands(e % 2, 2 + e // 2)
                        maxima(at + 2, at + 4)

        def xnT_copy(act, n):
            act.wait_ge(xnT_ps, n.u + 1)
            act.copy(xnT_next[:], ps[:, SIDE_BANK, :]).then_inc(xnT_ready, 1)

        def operand_copies(copy, wait, n, side, j):
            ps_done, copied, buf = ((q_ps, q_copied, QO), (k_ps, k_copied, KO))[side]
            bank = operand_bank(n, side, j)
            wait(ps_done, 4 * n.u + j + 1)
            for r in range(2):
                src = ps_bf(bank)[SLOT * r:SLOT * r + SLOT, :]
                heads = buf[0:SLOT, G * j:G * j + G]
                if n.L == 0:
                    src, dst = src.rearrange("p (i n) -> p i n", i=2), heads[:, r:G:2, :]
                else:
                    src = src.rearrange("p (i n) -> p i n", n=P)
                    dst = heads.rearrange("p h (t c) -> p c (h t)", c=H)[:, r:H:2, :]
                copy(dst, src).then_inc(copied, 1)

        def maxima_copy(act, w, s):
            act.wait_ge(mT_ps, STEPS * w.u + s + 1)
            act.copy(mT[:, s % 2, :], ps_bf(turned_max_bank(s))[0:3 * G, 0:S]).then_inc(mT_ready, 1)

        def exponential(act, w, s, i):
            act.wait_ge(st_ps, EXPS * (STEPS * w.u + s) + i + 1)
            if s > 0 or i >= 4:
                act.wait_ge(pv_done, NT * (STEPS * w.u + s) + i // 2 - 1)
            act.activation(PT[:, i % 4], ps[:, 2 * (i % 2):2 * (i % 2) + 2, :], ACT.Exp).then_inc(exp_done, 1)

        def output_copy(act, w, a):
            act.wait_ge(pv_done, NT * (STEPS * w.u + 2 * a + 2))
            act.copy(o_sb[:, a, :], ps[:, PV_BANK, :]).then_inc(o_copied, 1)

        def silu(act, w, i):
            L, NG = w.L, gate_ups(w.L)
            act.wait_ge(gate_ps[L], NG * w.b + i + 1)
            if i >= 2:
                act.wait_ge(h_ready[L], NG * w.b + i - 1)
            act.activation(sil[:, i % 2, :], ps[:, gu_bank(2 * i), :], ACT.Silu).then_inc(silu_done[L], 1)

        def onT_copy(act, w):
            act.wait_ge(onT_ps, w.u + 1)
            act.copy(o_T[:], ps[:, 4, :]).then_inc(onT_ready, 1)

        def scalar_unit(act, w, n):
            for s in range(STEPS):
                for i in range(EXPS):
                    exponential(act, w, s, i)
                    if (s, (i - 1) // 2) in TURNS and i % 2 == 1:
                        maxima_copy(act, w, s + 1)
                    if n is not None and (s, i) == (0, 7):
                        xnT_copy(act, n)
                    if (w.L, s, i) == (1, 2, 5):
                        act.wait_ge(lg_ready, w.b + 1)
                        act.activation(r_t[:, 1], r_t[:, 0], ACT.Exp).then_inc(rexp_done, 1)
                if s % 2 == 1:
                    output_copy(act, w, s // 2)

            def operands(side, j):
                if n is not None:
                    operand_copies(act.copy, act.wait_ge, n, side, j)

            silu(act, w, 0)
            silu(act, w, 1)
            silu(act, w, 2)
            if w.L == 0:
                operands(0, 2)
                operands(1, 2)
                onT_copy(act, w)
                operands(0, 3)
                operands(1, 3)
            else:
                onT_copy(act, w)
                silu(act, w, 3)
                for e in range(E - 2):
                    for i in range(EB):
                        silu(act, w, (e + 2) * EB + i)
                    if e < 4:
                        operands(e % 2, 2 + e // 2)
            if n is not None:
                maxima_copy(act, n, 0)

        def statistics(dve, n):
            dve.wait_ge(x_loaded, 16 * n.u + 16)
            for t in range(NT):
                last = dve.bn_stats(stats[:, t, :], x_next[:, t, :])
            last.then_inc(stats_done, 1)
            dve.wait_ge(stats_done, n.u + 1)
            dve.tensor_copy(wait_taker[:], eps_t[:])
            for t in range(NT):
                last = dve.bn_aggr(mv[:, t, :], stats[:, t, :])
            last.then_inc(mv_ready, 1)

        def normalize(dve, n):
            dve.wait_ge(rstd_ready, 2 * n.u + 2)
            for t in range(NT):
                last = dve.tensor_scalar(xn[:, t, :], x_next[:, t, :], mv[:, t, 0:1], rstd[:, t:t + 1],
                                         ALU.subtract, ALU.mult)
            last.then_inc(xn_ready, 1)

        def read_qkv(dve, n, t):
            dve.wait_ge(qkv_ps, NT * n.u + t + 1)
            bias = b_qkv[n.L]
            bank = qkv_bank(n, t)
            dve.tensor_tensor(qk[:, :, t, :], ps[:, bank, 0:2 * D].rearrange("p (i d) -> p i d", i=2),
                              bias[:, 0:2 * D].rearrange("p (i d) -> p i d", i=2), ALU.add)
            dve.tensor_tensor(v_nat[:, t, :], ps[:, bank, 2 * D:3 * D], bias[:, 2 * D:3 * D],
                              ALU.add).then_inc(qkv_read, 1)

        def slot_copy(eng, n, i, side):
            a, z, step = (((0, 3, 1), (2, 5, 1)), ((3, 6, 2), (1, 6, 4)), ((4, 5, 1), (0, 1, 1)))[i][side]
            slots = (Rq, Rk)[side][:, :, 0:48].rearrange("p n (s d) -> p n s d", d=HD)[:, :, a:z:step, :]
            return eng.tensor_copy(slots, part[i][:, side].unsqueeze(2).to_broadcast(
                [P, NT * H, len(range(a, z, step)), HD]))

        def split_qk(dve, n):
            flat = [t[:].rearrange("p q t d -> p (q t d)") for t in (qk, rest[0], rest[1])]
            parts = [t[:].rearrange("p q n d -> p (q n d)") for t in part]
            dve.wait_ge(qkv_read, NT * n.u + NT)
            for i in range(3):
                done = (p1_ready, p2_ready, p3_ready)[i]
                dve.tensor_copy(parts[i], flat[i]).then_inc(done, 1)
                dve.wait_ge(done, n.u + 1)
                if i < 2:
                    left = (r1_ready, r2_ready)[i]
                    dve.tensor_tensor(flat[i + 1], flat[i], parts[i], ALU.subtract).then_inc(left, 1)
                    dve.wait_ge(left, n.u + 1)
            for i, side in ((0, 0), (0, 1), (1, 0), (1, 1), (2, 1)):
                slot_copy(dve, n, i, side).then_inc(R1_ready, 1)

        def read_max(dve, w, s, i):
            dve.wait_ge(max_ps, MAXES * (STEPS * w.u + s) + i + 1)
            dve.tensor_reduce(mx[:, s % 2].rearrange("p t g -> p (t g)")[:, i:i + 1],
                              ps[:, max_bank(s, i), :], AX_X, ALU.max).then_inc(max_read, 1)

        def split_max(dve, w, s):
            m, r, p = mx[:, s % 2], mr[:, s % 2], mp[:, s % 2]
            base = 4 * (STEPS * w.u + s)
            dve.wait_ge(max_read, MAXES * (STEPS * w.u + s + 1))
            if s >= 2:
                dve.wait_ge(mT_ps, STEPS * w.u + s - 1)
            dve.tensor_scalar(p[:, :, 0, :], m, -1.0, None, ALU.mult).then_inc(m_chain, 1)
            dve.wait_ge(m_chain, base + 1)
            dve.scalar_tensor_tensor(out=r, in0=m, scalar=-1.0, in1=p[:, :, 0, :], op0=ALU.mult,
                                     op1=ALU.subtract).then_inc(m_chain, 1)
            dve.wait_ge(m_chain, base + 2)
            dve.tensor_copy(p[:, :, 1, :], r).then_inc(m_chain, 1)
            dve.wait_ge(m_chain, base + 3)
            dve.tensor_tensor(r, r, p[:, :, 1, :], ALU.subtract).then_inc(m_chain, 1)
            dve.wait_ge(m_chain, base + 4)
            dve.tensor_copy(p[:, :, 2, :], r).then_inc(m_split, 1)

        def attention_out(dve, w):
            dve.wait_ge(oT_ps, w.u + 1)
            oT = ps[:, 4:6, :].rearrange("p k (n f) -> p (k n) f", f=P)
            dve.reciprocal(rden[:], oT.rearrange("p n (g f) -> p n g f", g=G)[:, :, :, 16:18]).then_inc(rden_ready, 1)
            dve.wait_ge(rden_ready, w.u + 1)
            for a in range(2):
                for c in range(2):
                    src = oT.rearrange("p (t a) (g f) -> p a t g f", a=2, g=G)[:, a, :, :, HD * c:HD * c + HD]
                    dst = o_nat[:].rearrange("p t (s g d) -> p s t g d", g=G, d=HD)[:, 2 * a + c]
                    den = rden[:].rearrange("p (t a) g c -> p a c t g", a=2)[:, a, c]
                    last = dve.tensor_tensor(dst, src, den.unsqueeze(3).to_broadcast([P, NT, G, HD]), ALU.mult)
            last.then_inc(on_ready, 1)

        def gated(dve, w, i):
            L, NG = w.L, gate_ups(w.L)
            dve.wait_ge(up_ps[L], NG * w.b + i + 1)
            dve.wait_ge(silu_done[L], NG * w.b + i + 1)
            if L == 1 and i >= 2 * EB and i % EB == 0:
                dve.wait_ge(y_ps[1], (E + 1) * w.b + i // EB)
            dst = hT[:, 0, i, :] if L == 0 else hT[:, (i // EB) % 2, i % EB, :]
            dve.tensor_tensor(dst, ps[:, gu_bank(2 * i + 1), :], sil[:, i % 2, :], ALU.mult).then_inc(h_ready[L], 1)

        def chain(dve, sem_, base):
            links = [0]

            def link(ins):
                links[0] += 1
                ins.then_inc(sem_, 1)
                dve.wait_ge(sem_, base + links[0])
            return link, links

        def wide(v):
            return v.unsqueeze(2).to_broadcast([P, NT, E])

        def read_logits(dve, w, link):
            dve.wait_ge(logit_ps, w.b + 1)
            lg = ps[:, LOGIT_BANK, 0:NT * E].rearrange("p (t e) -> p t e", e=E)
            link(dve.tensor_reduce(r_s[:, 0], lg, AX_X, ALU.max))
            dve.tensor_tensor(r_t[:, 0], lg, wide(r_s[:, 0]), ALU.subtract).then_inc(lg_ready, 1)

        def choose_experts(dve, w, link):
            dve.wait_ge(rexp_done, w.b + 1)
            link(dve.tensor_reduce(r_s[:, 0], r_t[:, 1], AX_X, ALU.add))
            link(dve.reciprocal(r_s[:, 1], r_s[:, 0]))
            link(dve.tensor_tensor(r_p[:], r_t[:, 1], wide(r_s[:, 1]), ALU.mult))
            for k in range(2):
                link(dve.tensor_reduce(r_s[:, 2 + k], r_p[:], AX_X, ALU.max))
                link(dve.tensor_tensor(r_t[:, 2], r_p[:], wide(r_s[:, 2 + k]), ALU.is_equal))
                link(dve.scalar_tensor_tensor(out=r_t[:, 3], in0=r_t[:, 2], scalar=-99.0, in1=iota_hi[:],
                                              op0=ALU.mult, op1=ALU.add))
                link(dve.tensor_reduce(r_s[:, 4], r_t[:, 3], AX_X, ALU.min))
                link(dve.tensor_tensor(oh[:, :, k, :], iota_e[:], wide(r_s[:, 4]), ALU.is_equal))
                if k == 0:
                    link(dve.scalar_tensor_tensor(out=r_p[:], in0=oh[:, :, 0, :], scalar=-2.0, in1=r_p[:],
                                                  op0=ALU.mult, op1=ALU.add))
            dve.tensor_tensor(r_s[:, 0], r_s[:, 2], r_s[:, 3], ALU.add).then_inc(oh_ready, 1)
            dve.wait_ge(oh_ready, w.b + 1)
            link(dve.tensor_scalar(r_s[:, 1], r_s[:, 0], 1e-9, None, ALU.add))
            link(dve.reciprocal(r_s[:, 0], r_s[:, 1]))
            link(dve.tensor_tensor(r_s[:, 5:7], r_s[:, 2:4], r_s[:, 0:1].to_broadcast([P, 2, NT]), ALU.mult))

        def combine_weights(dve, w, link):
            dve.wait_ge(rank_ps, w.b + 1)
            NK = 2 * E
            link(dve.tensor_copy(tot[:].rearrange("p t k -> p (t k)"), ps[:, ROUTER_BANK, 128:128 + NT * NK]))
            for t in range(NT):
                link(dve.tensor_tensor(rk[:, t, :], ps[:, ROUTER_BANK, 64 + t * NK:64 + (t + 1) * NK],
                                       carry[:, t % 2, :], ALU.add))
                link(dve.tensor_tensor(carry[:, (t + 1) % 2, :], carry[:, t % 2, :], tot[:, t, :], ALU.add))
            rk4 = rk[:].rearrange("p t (k e) -> p t k e", e=E)
            for k in range(2):
                link(dve.tensor_scalar(r_t[:, 2], rk4[:, :, k, :], float(CAP), None, ALU.is_le))
                link(dve.tensor_tensor(r_t[:, 3], r_t[:, 2], oh[:, :, k, :], ALU.mult))
                dst = comb[:] if k == 0 else r_t[:, 0]
                link(dve.tensor_tensor(dst, r_t[:, 3], wide(r_s[:, 5 + k]), ALU.mult))
            link(dve.tensor_tensor(comb[:], comb[:], r_t[:, 0], ALU.add))

        def residual(dve, w, bank):
            dve.wait_ge(stored, 16 * w.u + 16)
            dve.wait_ge(x_taken, 2 * w.u + 2)
            return dve.tensor_tensor(x_out[:], ps[:, bank, :].rearrange("p (t d) -> p t d", d=D), x_in[:], ALU.add)

        def first_maxima_read(dve, n, i):
            if n is not None:
                read_max(dve, n, i // MAXES, i % MAXES)
                if i % MAXES == MAXES - 1:
                    split_max(dve, n, i // MAXES)

        def vector_unit(dve, w, n):
            for s in range(2, STEPS):
                for k in range(NT):
                    for g in range(G):
                        read_max(dve, w, s, G * k + g)
                    if n is not None:
                        if (s, k) == (2, 1):
                            statistics(dve, n)
                        if (s, k) == (2, 2):
                            normalize(dve, n)
                        if s == 3 and k >= 1:
                            read_qkv(dve, n, k - 1)
                split_max(dve, w, s)
            if w.L == 1:
                link, links = chain(dve, route_chain, ROUTE_LINKS * w.b)
                read_logits(dve, w, link)
            if n is not None:
                read_qkv(dve, n, 3)
                split_qk(dve, n)
                if (w.L, n.L) == (0, 1):
                    setup_vector(dve)
            if w.L == 1:
                choose_experts(dve, w, link)
            if n is not None:
                for j in range(2):
                    for side in range(2):
                        operand_copies(dve.tensor_copy, dve.wait_ge, n, side, j)

            def maxima(a, z):
                for i in range(a, z):
                    first_maxima_read(dve, n, i)

            gated(dve, w, 0)
            maxima(0, 2)
            attention_out(dve, w)
            gated(dve, w, 1)
            if w.L == 0:
                maxima(2, 7)
                gated(dve, w, 2)
                maxima(7, 25)
                dve.wait_ge(y_ps[0], w.b + 1)
                residual(dve, w, 5).then_inc(unit_done, 1)
                maxima(25, 32)
            else:
                maxima(2, 4)
                gated(dve, w, 2)
                maxima(4, 8)
                gated(dve, w, 3)
                combine_weights(dve, w, link)
                assert links[0] == ROUTE_LINKS, links[0]
                dve.wait_ge(y_ps[1], (E + 1) * w.b + 1)
                residual(dve, w, 5).then_inc(y_read, 1)
                for e in range(E):
                    at = 8 + 4 * e
                    if e + 2 < E:
                        gated(dve, w, (e + 2) * EB)
                    dve.wait_ge(y_ps[1], (E + 1) * w.b + e + 2)
                    dve.wait_ge(y_read, E * w.b + e + 1)
                    for t in range(NT):
                        last = dve.scalar_tensor_tensor(
                            out=x_out[:, t, :], in0=ps[:, 4 + e % 2, t * P:(t + 1) * P],
                            scalar=comb[:, t, e:e + 1], in1=x_out[:, t, :], op0=ALU.mult, op1=ALU.add)
                    last.then_inc(y_read if e + 1 < E else unit_done, 1)
                    if e + 2 < E:
                        maxima(at, at + 2)
                        gated(dve, w, (e + 2) * EB + 1)
                        maxima(at + 2, at + 4)

        def all_units(eng, unit):
            with eng.Fori(0, B - 1) as b:
                unit(eng, Unit(0, b), Unit(0, b + 1))
            unit(eng, Unit(0, B - 1), Unit(1, 0, beside=0))
            with eng.Fori(0, B - 1) as b:
                unit(eng, Unit(1, b), Unit(1, b + 1))
            unit(eng, Unit(1, B - 1), None)

        block = ctx.enter_context(nc.Block())

        @block.sync
        def _(sp):
            load_x(sp, FIRST)
            first_setup_sync(sp)
            setup_sync(sp)
            sp.sem_inc(unit_done, 1)
            sp.sem_inc(stored, 16)
            sp.wait_ge(consts, N_CONST)
            sp.wait_ge(operands_cleared, 2)
            sp.dma_start(KO[MASK_ROW:MASK_ROW + NB, :, :],
                         onehot_k[:].unsqueeze(1).to_broadcast([NB, H, S])).then_inc(key_rows_in, 16)
            max_rows_in(sp, FIRST, 0)
            with sp.Fori(0, B - 1) as b:
                sync_unit(sp, Unit(0, b), Unit(0, b + 1))
            w, n = Unit(0, B - 1), Unit(1, 0, beside=0)
            sp.wait_ge(x_taken, 2 * w.u + 2)
            load_x(sp, n)
            for s in range(1, STEPS):
                max_rows_in(sp, w, s)
            sp.wait_ge(pv_done, NT * STEPS * n.u)
            sp.wait_ge(mask_ready, 1)
            sp.dma_start(QO[MASK_ROW:MASK_ROW + NB, :, :],
                         mask_q[:].unsqueeze(1).to_broadcast([NB, H, S])).then_inc(rows_in, 16)
            place_values_1(sp, n)
            store_x(sp, w)
            max_rows_in(sp, n, 0)
            with sp.Fori(0, B - 1) as b:
                sync_unit(sp, Unit(1, b), Unit(1, b + 1))
            sync_unit(sp, Unit(1, B - 1), None)
            sp.wait_ge(stored, 16 * 2 * B + 16)

        @block.gpsimd
        def _(pool):
            first_setup_pool(pool)
            reciprocal_deviation(pool, FIRST)
            setup_pool(pool)
            fill_slots(pool, FIRST)
            place_values_0(pool, FIRST)
            dequantize(pool)
            all_units(pool, pool_unit)

        @block.vector
        def _(dve):
            dve.wait_ge(zeros, N_ZERO)
            statistics(dve, FIRST)
            normalize(dve, FIRST)
            first_setup_vector(dve)
            for t in range(NT):
                read_qkv(dve, FIRST, t)
            dve.wait_ge(cleared, N_CLEARED)
            split_qk(dve, FIRST)
            for j in range(2):
                for side in range(2):
                    operand_copies(dve.tensor_copy, dve.wait_ge, FIRST, side, j)
            for i in range(2 * MAXES):
                first_maxima_read(dve, FIRST, i)
            all_units(dve, vector_unit)

        @block.scalar
        def _(act):
            setup_scalar(act)
            xnT_copy(act, FIRST)
            for j in range(2, 4):
                for side in range(2):
                    operand_copies(act.copy, act.wait_ge, FIRST, side, j)
            maxima_copy(act, FIRST, 0)
            all_units(act, scalar_unit)

        @block.tensor
        def _(pe):
            pe.wait_ge(consts, N_IDENT)
            xnT_mms(pe, FIRST)
            pe.wait_ge(first_ready, 1)
            for t in range(NT):
                qkv_mm(pe, FIRST, t)
            pe.wait_ge(consts, N_CONST)
            pe.wait_ge(cleared, N_CLEARED)
            for j in range(2):
                for side in range(2):
                    operand_transposes(pe, FIRST, side, j)
            pe.wait_ge(key_rows_in, 16)
            for i in range(2 * MAXES):
                if i % 6 == 2 and i < 24:
                    operand_transposes(pe, FIRST, i // 6 % 2, 2 + i // 12)
                first_maxima(pe, FIRST, i)
            with pe.Fori(0, B - 1) as b:
                tensor_unit(pe, Unit(0, b), Unit(0, b + 1))
            tensor_unit(pe, Unit(0, B - 1), Unit(1, 0, beside=0))
            with pe.Fori(0, B - 1) as b:
                tensor_unit(pe, Unit(1, b), Unit(1, b + 1))
            tensor_unit(pe, Unit(1, B - 1), None)


def kernel(L0_attn_x, L0_attn_qkv_w, L0_attn_qkv_b, L0_attn_proj_w, L0_attn_proj_b, L0_ffn_w_gate, L0_ffn_w_up,
           L0_ffn_w_down, L1_attn_Wq, L1_attn_bq, L1_attn_Wk, L1_attn_bk, L1_attn_Wv, L1_attn_bv, L1_attn_Wo,
           L1_attn_bo, L1_attn_src_blocks, L1_attn_tgt_blocks, L1_ffn_gate_w, L1_ffn_gate_proj_w,
           L1_ffn_up_proj_w, L1_ffn_down_proj_w):
    import numpy as np
    import concourse.bacc as bacc
    from concourse.bass_utils import run_bass_kernel_spmd

    def T(a, *axes):
        return np.ascontiguousarray(np.transpose(np.asarray(a), axes or None))

    arrays = {
        "x": np.asarray(L0_attn_x),
        "qkv_wT": T(L0_attn_qkv_w), "qkv_b": np.asarray(L0_attn_qkv_b),
        "proj_wT": T(L0_attn_proj_w), "proj_b": np.asarray(L0_attn_proj_b),
        "wg_T": T(L0_ffn_w_gate), "wu_T": T(L0_ffn_w_up), "wd_T": T(L0_ffn_w_down),
        "Wq_T": T(L1_attn_Wq), "bq": np.asarray(L1_attn_bq),
        "Wk_T": T(L1_attn_Wk), "bk": np.asarray(L1_attn_bk),
        "Wv_T": T(L1_attn_Wv), "bv": np.asarray(L1_attn_bv),
        "Wo_T": T(L1_attn_Wo), "bo": np.asarray(L1_attn_bo),
        "src_blocks": np.asarray(L1_attn_src_blocks), "tgt_blocks": np.asarray(L1_attn_tgt_blocks),
        "router_T": T(L1_ffn_gate_w),
        "eg_T": T(L1_ffn_gate_proj_w, 2, 0, 1), "eu_T": T(L1_ffn_up_proj_w, 2, 0, 1),
        "ed_T": T(L1_ffn_down_proj_w, 0, 2, 1),
    }
    nc = bacc.Bacc("TRN2", target_bir_lowering=False, num_devices=1)
    args = {n: nc.dram_tensor("in_" + n, a.shape, mybir.dt.from_np(a.dtype), kind="ExternalInput").ap()
            for n, a in arrays.items()}
    out = nc.dram_tensor("out_y", arrays["x"].shape, F32, kind="ExternalOutput").ap()
    build(nc, out=out, **args)
    r = run_bass_kernel_spmd(nc, [{"in_" + n: a for n, a in arrays.items()}], core_ids=[0])
    return r.results[0]["out_y"]
```
